# Optimizing a Trainium2 kernel written in Bass

```python
import numpy as np
import jax
import jax.numpy as jnp

def _softmax(x, axis=-1):
    return jax.nn.softmax(x, axis=axis)

def _gelu(x):
    return jax.nn.gelu(x, approximate=True)

def _silu(x):
    return jax.nn.silu(x)

def _sigmoid(x):
    return jax.nn.sigmoid(x)

def _layernorm(x, axis=-1, eps=1e-05):
    m = jnp.mean(x, axis=axis, keepdims=True)
    v = jnp.var(x, axis=axis, keepdims=True)
    return (x - m) / jnp.sqrt(v + eps)

def _scatter_add(tgt, idx, src, axis=0):
    return tgt.at[idx].add(src)

def _segment_sum(src, seg, n):
    return jax.ops.segment_sum(src, seg, n)
kernel_name = 'mk_vit_tower_d1_tok_img256_r4_82d0b5'

def setup_inputs(seed: int=0):
    np.random.seed(seed)
    _w = jnp.asarray

    def _rec_inputs():
        import jax
        import jax.numpy as jnp
        _rk = jax.random.key(seed)
        x = -0.000798584 + 1.00089 * jax.random.normal(jax.random.fold_in(_rk, 1), (128, 64, 75, 3), jnp.float32)
        return x
    x = _rec_inputs()

    def _L0_tok_setup():
        import jax, jax.numpy as jnp
        import numpy as np
        EPS = 1e-05
        B, T, V = (32, 64, 75)
        DIMS = [3, 128, 128, 64]

        def _layer(x, A, W, b, g, be, m, v, relu):
            x = jnp.einsum('btvc,co->btvo', x, W)
            x = jnp.einsum('uv,btvo->btuo', A, x)
            x = x + b
            x = (x - m) * (g * jax.lax.rsqrt(v + EPS)) + be
            if relu:
                x = jax.nn.relu(x)
            return x
        key = jax.random.key(seed)
        ks = jax.random.split(key, 32)
        inp = {'x': jax.random.normal(ks[0], (B, T, V, DIMS[0]), dtype=jnp.float32), 'A': jax.random.uniform(ks[1], (V, V), dtype=jnp.float32) / V}
        ki = 2
        for i in range(3):
            cin, cout = (DIMS[i], DIMS[i + 1])
            bound = float(np.sqrt(6.0 / (cin + cout)))
            inp[f'W{i}'] = jax.random.uniform(ks[ki], (cin, cout), minval=-bound, maxval=bound, dtype=jnp.float32)
            ki += 1
            inp[f'b{i}'] = jnp.zeros((cout,), dtype=jnp.float32)
            inp[f'g{i}'] = jnp.ones((cout,), dtype=jnp.float32)
            inp[f'be{i}'] = jnp.zeros((cout,), dtype=jnp.float32)
            inp[f'm{i}'] = 0.1 * jax.random.normal(ks[ki], (cout,), dtype=jnp.float32)
            ki += 1
            inp[f'v{i}'] = jax.random.uniform(ks[ki], (cout,), minval=0.5, maxval=1.5, dtype=jnp.float32)
            ki += 1
        return inp
    _L0_tok_all = _L0_tok_setup()
    _L0_tok_in = {k: v for k, v in _L0_tok_all.items() if k in ('A', 'W0', 'b0', 'g0', 'be0', 'm0', 'v0', 'W1', 'b1', 'g1', 'be1', 'm1', 'v1', 'W2', 'b2', 'g2', 'be2', 'm2', 'v2')}
    del _L0_tok_all

    def _L0_attn_setup():
        import jax, jax.numpy as jnp
        import numpy as np
        B, L, D = (4, 1024, 64)
        key = jax.random.key(seed)
        kx, kq, kk, kv, ko = jax.random.split(key, 5)
        std = 0.02
        return {'x': jax.random.normal(kx, (B, L, D), dtype=jnp.float32), 'Wq': std * jax.random.normal(kq, (D, D), dtype=jnp.float32), 'Wk': std * jax.random.normal(kk, (D, D), dtype=jnp.float32), 'Wv': std * jax.random.normal(kv, (D, D), dtype=jnp.float32), 'Wo': std * jax.random.normal(ko, (D, D), dtype=jnp.float32)}
    _L0_attn_all = _L0_attn_setup()
    _L0_attn_in = {k: v for k, v in _L0_attn_all.items() if k in ('Wq', 'Wk', 'Wv', 'Wo')}
    del _L0_attn_all

    def _L0_ffn_setup():
        import jax, jax.numpy as jnp
        import numpy as np
        TOP_K = 2
        key = jax.random.key(seed)
        ks = jax.random.split(key, 4)
        B, L, D, H, E = (8, 1024, 64, 256, 8)
        s = 0.02
        return {'x': jax.random.normal(ks[0], (B, L, D), jnp.float32), 'Wg': jax.random.normal(ks[1], (D, E), jnp.float32) * s, 'bg': jnp.zeros((E,), jnp.float32), 'W1': jax.random.normal(ks[2], (E, D, H), jnp.float32) * s, 'b1': jnp.zeros((E, H), jnp.float32), 'W2': jax.random.normal(ks[3], (E, H, D), jnp.float32) * s, 'b2': jnp.zeros((E, D), jnp.float32)}
    _L0_ffn_all = _L0_ffn_setup()
    _L0_ffn_in = {k: v for k, v in _L0_ffn_all.items() if k in ('Wg', 'bg', 'W1', 'b1', 'W2', 'b2')}
    del _L0_ffn_all
    return {'x': x, 'L0_tok_A': _L0_tok_in['A'], 'L0_tok_W0': _L0_tok_in['W0'], 'L0_tok_b0': _L0_tok_in['b0'], 'L0_tok_g0': _L0_tok_in['g0'], 'L0_tok_be0': _L0_tok_in['be0'], 'L0_tok_m0': _L0_tok_in['m0'], 'L0_tok_v0': _L0_tok_in['v0'], 'L0_tok_W1': _L0_tok_in['W1'], 'L0_tok_b1': _L0_tok_in['b1'], 'L0_tok_g1': _L0_tok_in['g1'], 'L0_tok_be1': _L0_tok_in['be1'], 'L0_tok_m1': _L0_tok_in['m1'], 'L0_tok_v1': _L0_tok_in['v1'], 'L0_tok_W2': _L0_tok_in['W2'], 'L0_tok_b2': _L0_tok_in['b2'], 'L0_tok_g2': _L0_tok_in['g2'], 'L0_tok_be2': _L0_tok_in['be2'], 'L0_tok_m2': _L0_tok_in['m2'], 'L0_tok_v2': _L0_tok_in['v2'], 'L0_attn_Wq': _L0_attn_in['Wq'], 'L0_attn_Wk': _L0_attn_in['Wk'], 'L0_attn_Wv': _L0_attn_in['Wv'], 'L0_attn_Wo': _L0_attn_in['Wo'], 'L0_ffn_Wg': _L0_ffn_in['Wg'], 'L0_ffn_bg': _L0_ffn_in['bg'], 'L0_ffn_W1': _L0_ffn_in['W1'], 'L0_ffn_b1': _L0_ffn_in['b1'], 'L0_ffn_W2': _L0_ffn_in['W2'], 'L0_ffn_b2': _L0_ffn_in['b2']}

def reference(x, L0_tok_A, L0_tok_W0, L0_tok_b0, L0_tok_g0, L0_tok_be0, L0_tok_m0, L0_tok_v0, L0_tok_W1, L0_tok_b1, L0_tok_g1, L0_tok_be1, L0_tok_m1, L0_tok_v1, L0_tok_W2, L0_tok_b2, L0_tok_g2, L0_tok_be2, L0_tok_m2, L0_tok_v2, L0_attn_Wq, L0_attn_Wk, L0_attn_Wv, L0_attn_Wo, L0_ffn_Wg, L0_ffn_bg, L0_ffn_W1, L0_ffn_b1, L0_ffn_W2, L0_ffn_b2):
    import jax
    import jax.numpy as jnp

    def _L0_tok_ref(x, A, W0, b0, g0, be0, m0, v0, W1, b1, g1, be1, m1, v1, W2, b2, g2, be2, m2, v2):
        import jax, jax.numpy as jnp
        import numpy as np
        EPS = 1e-05
        B, T, V = (32, 64, 75)
        DIMS = [3, 128, 128, 64]

        def _layer(x, A, W, b, g, be, m, v, relu):
            x = jnp.einsum('btvc,co->btvo', x, W)
            x = jnp.einsum('uv,btvo->btuo', A, x)
            x = x + b
            x = (x - m) * (g * jax.lax.rsqrt(v + EPS)) + be
            if relu:
                x = jax.nn.relu(x)
            return x
        x = _layer(x, A, W0, b0, g0, be0, m0, v0, relu=True)
        x = _layer(x, A, W1, b1, g1, be1, m1, v1, relu=True)
        x = _layer(x, A, W2, b2, g2, be2, m2, v2, relu=False)
        return x.mean(axis=2)

    def _L0_attn_ref(x, Wq, Wk, Wv, Wo):
        import jax, jax.numpy as jnp
        import numpy as np
        B, L, D = (4, 1024, 64)
        q = x @ Wq.T
        k = x @ Wk.T
        v = x @ Wv.T
        logits = jnp.einsum('bld,bmd->blm', q, k)
        Lq = x.shape[1]
        causal_mask = jnp.triu(jnp.ones((Lq, Lq), dtype=bool), k=1)
        logits = jnp.where(causal_mask[None], jnp.asarray(0.0, logits.dtype), logits)
        attn = jax.nn.relu(logits)
        row_counts = jnp.maximum(jnp.arange(Lq, dtype=attn.dtype), 1.0)
        attn = attn / row_counts[None, :, None]
        ctx = jnp.einsum('blm,bmd->bld', attn, v)
        return ctx @ Wo.T

    def _L0_ffn_ref(x, Wg, bg, W1, b1, W2, b2):
        import jax, jax.numpy as jnp
        import numpy as np
        TOP_K = 2
        B, L, D = x.shape
        E = W1.shape[0]
        xf = x.reshape(-1, D)
        gate_logits = xf @ Wg + bg
        top_w, top_i = jax.lax.top_k(gate_logits, TOP_K)
        top_w = jax.nn.softmax(top_w, axis=-1)
        w_dense = jnp.sum(jax.nn.one_hot(top_i, E, dtype=xf.dtype) * top_w[..., None], axis=1)
        out = jnp.zeros_like(xf)
        for e in range(E):
            h = jax.nn.gelu(xf @ W1[e] + b1[e], approximate=False)
            out = out + w_dense[:, e:e + 1] * (h @ W2[e] + b2[e])
        return out.reshape(B, L, D)
    h = _L0_tok_ref(x, L0_tok_A, L0_tok_W0, L0_tok_b0, L0_tok_g0, L0_tok_be0, L0_tok_m0, L0_tok_v0, L0_tok_W1, L0_tok_b1, L0_tok_g1, L0_tok_be1, L0_tok_m1, L0_tok_v1, L0_tok_W2, L0_tok_b2, L0_tok_g2, L0_tok_be2, L0_tok_m2, L0_tok_v2)
    h = h + _L0_attn_ref(_layernorm(h, axis=-1), L0_attn_Wq, L0_attn_Wk, L0_attn_Wv, L0_attn_Wo)
    h = h + _L0_ffn_ref(_layernorm(h, axis=-1), L0_ffn_Wg, L0_ffn_bg, L0_ffn_W1, L0_ffn_b1, L0_ffn_W2, L0_ffn_b2)
    return h

_drawn_inputs = setup_inputs


def setup_inputs(seed=0):
    import zlib

    import numpy as np

    out = dict(_drawn_inputs(seed))
    spreads = {'L0_tok_b0': (0.0, 0.1),
     'L0_tok_g0': (1.0, 0.6),
     'L0_tok_be0': (0.0, 0.1),
     'L0_tok_b1': (0.0, 0.394),
     'L0_tok_g1': (1.0, 0.2),
     'L0_tok_be1': (0.0, 0.528),
     'L0_tok_b2': (0.0, 0.8),
     'L0_tok_g2': (1.0, 0.2),
     'L0_tok_be2': (0.0, 0.8),
     'L0_ffn_bg': (0.0, 0.8),
     'L0_ffn_b1': (0.0, 0.8),
     'L0_ffn_b2': (0.0, 2.0)}
    factors = {'x': 5.216,
     'L0_tok_A': 8.0,
     'L0_tok_W0': 4.272,
     'L0_tok_v0': 2.949,
     'L0_tok_m2': 8.0,
     'L0_attn_Wq': 8.0,
     'L0_attn_Wk': 8.0,
     'L0_attn_Wv': 8.0,
     'L0_attn_Wo': 8.0,
     'L0_ffn_Wg': 8.0,
     'L0_ffn_W1': 8.0,
     'L0_ffn_W2': 8.0}
    for name, (base, spread) in spreads.items():
        noise = np.random.default_rng([zlib.crc32(name.encode()), seed]).standard_normal(out[name].shape)
        drawn = base * np.exp(spread * noise) if base else spread * noise
        out[name] = jnp.asarray(drawn.astype(out[name].dtype))
    for name, factor in factors.items():
        out[name] = (out[name] * factor).astype(out[name].dtype)
    return out
```

```python
from contextlib import ExitStack

import numpy as np

import concourse.bass as bass
from concourse import mybir

F32 = mybir.dt.float32
F16 = mybir.dt.float16
U32 = mybir.dt.uint32
ALU = mybir.AluOpType
ACT = mybir.ActivationFunctionType
X = mybir.AxisListType.X

P = 128
EPS = 1e-5
B, T, V, CIN = 128, 64, 75, 3
C = 128
D = 64
E, H = 8, 256
TOKENS = B * T

FRAMES = 5
BLOCK = 125
BLOCKS = FRAMES * V // BLOCK
GROUP = FRAMES * V
GROUPS = 8
HALF = GROUPS // 2 * FRAMES
STEP = 2 * HALF
ITERS = -(-TOKENS // STEP)
PADDED = ITERS * STEP
XCOLS = 2 * CIN * HALF
XLOADS = 10
YROWS = 4 * CIN + 2
SPANS = [[(0, 75, 0, 0), (75, 50, 0, 1)],
         [(0, 25, 50, 0), (25, 75, 0, 1), (100, 25, 0, 2)],
         [(0, 50, 25, 0), (50, 75, 0, 1)]]
FIRST_FRAME = [0, 1, 3]
ABASE = [0, 2 * V, 5 * V]
ACOLS = 7 * V
YTOP, HTOP, ATOP = 2.0 ** 8, 2.0 ** 14, 2.0 ** 14
TINY = 2.0 ** -60
SLACK = 1.001

TILE = 128
QUAD = 4
QTOK = QUAD * TILE
QUADS = TOKENS // QTOK
TILES = TOKENS // TILE
PAIR = 2 * TILE


def build(nc, dram, out):
    ctx = ExitStack()
    with ctx:
        def sb(name, shape, dt=F32):
            return ctx.enter_context(nc.sbuf_tensor(name, shape, dt))

        def sem(name):
            return ctx.enter_context(nc.semaphore(name))

        bank = [ctx.enter_context(nc.psum_tensor(f"bank{n}", [P, 512], F32)) for n in range(8)]

        xs = sb("xs", [P, PADDED * CIN])
        hbar = sb("hbar", [P, PADDED])
        ident = sb("ident", [P, P])
        ident16 = sb("ident16", [P, P], F16)
        causal = sb("causal", [P, P])
        iota8 = sb("iota8", [P, E])
        at32 = sb("at32", [V, V])
        a32 = sb("a32", [V, V])
        w0t = sb("w0t", [P, CIN])
        bn0 = sb("bn0", [P, 5])
        bn1 = sb("bn1", [P, 5])
        bn1row = sb("bn1row", [P, 5, C])
        bn2row = sb("bn2row", [P, 5, D])
        w1 = sb("w1", [P, C])
        w2 = sb("w2", [P, D])
        wq = sb("wq", [D, D])
        wk = sb("wk", [D, D])
        wv = sb("wv", [D, D])
        wot = sb("wot", [D, D])
        wg = sb("wg", [D + 1, E])
        ew1 = sb("ew1", [D + 1, E * H])
        ew2 = sb("ew2", [P, 2 * E, D])
        eb2 = sb("eb2", [P, E * D])
        stat = sb("stat", [P, 2])
        top = sb("top", [P, 2])
        xmax = sb("xmax", [P, XLOADS])
        col = sb("col", [P, 40])
        w4 = sb("w4", [P, 4])
        w4hi = sb("w4hi", [P, 4], F16)
        w4lo = sb("w4lo", [P, 4], F16)
        w0cols = sb("w0cols", [P, YROWS], F16)
        w0x = sb("w0x", [YROWS, C], F16)
        ascaled = sb("ascaled", [V, V])
        ahi = sb("ahi", [V, V], F16)
        alo = sb("alo", [V, V], F16)
        ablkhi = sb("ablkhi", [P, ACOLS], F16)
        ablklo = sb("ablklo", [P, ACOLS], F16)
        vareps = sb("vareps", [P, 2 + C + D])
        root = sb("root", [P, 2 + C + D])
        newton = sb("newton", [P, 2 + C + D])
        g1row = sb("g1row", [P, C])
        w1s = sb("w1s", [P, C])
        g2row = sb("g2row", [P, D])
        w2s = sb("w2s", [P, D])
        ones = sb("ones", [P, P])
        abar = sb("abar", [P, FRAMES, V])
        corr = sb("corr", [P, P])
        bias2 = sb("bias2", [P, D])
        mqk = sb("mqk", [D, D])
        nvo = sb("nvo", [D, D])
        xcur = sb("xcur", [V, XCOLS])
        yhi = sb("yhi", [XCOLS, V], F16)
        ylo = sb("ylo", [XCOLS, V], F16)
        yt = sb("yt", [YROWS, STEP * V], F16)
        h0hi = sb("h0hi", [BLOCK, 2, BLOCKS * C], F16)
        h0lo = sb("h0lo", [BLOCK, 2, BLOCKS * C], F16)
        pt = sb("pt", [P, 2, GROUP])
        q = sb("q", [P, 2, GROUP])

        at = 0

        def again(cols, rows=P):
            nonlocal at
            view = xs[0:rows, at:at + cols]
            at += cols
            return view

        h2all = again(TILES * D)
        xn2t = again(TOKENS, D + 1)
        hb = again(QTOK)
        hs = again(QUAD * D)
        bn = again(QUAD * 6)
        mv = again(QUAD * 2)
        ve = again(QUAD)
        rstd = again(QUAD)
        nt = again(QUAD)
        xn = again(QUAD * D)
        xnt = again(QTOK, D)
        st = again(QTOK, D)
        vo = again(QUAD * D)
        attn = again(QTOK)
        h2 = again(QUAD * D)
        xn2 = again(QUAD * D)
        xn2q = again(QTOK, D + 1)
        gl = again(QUAD * E)
        mx = again(QUAD * 8)
        mi = again(QUAD * 8).bitcast(U32)
        best = again(TILES * 2)
        which = again(TILES * 2)
        gap = again(TILES)
        egap = again(TILES)
        prob = again(2 * TILES)
        den = again(TILES)
        hit = again(TILES * E)
        wd = again(TILES * E)
        gelu = again(2 * QTOK)
        ycomb = again(2 * E * D)
        osum = again(2 * QUAD * D)
        ofin = again(2 * QUAD * D)
        assert at <= PADDED * CIN

        s_par = sem("s_par")
        s_late = sem("s_late")
        x_in = [sem(f"x_in{n}") for n in range(XLOADS)]
        s_chain = sem("s_chain")
        s_stat = sem("s_stat")
        s_top = sem("s_top")
        s_asplit = sem("s_asplit")
        s_ablk = sem("s_ablk")
        s_w0c = sem("s_w0c")
        s_w0t = sem("s_w0t")
        s_w0x = sem("s_w0x")
        s_ones = sem("s_ones")
        s_abar = sem("s_abar")
        s_set = sem("s_set")
        s_var = sem("s_var")
        s_root = sem("s_root")
        s_corr = sem("s_corr")
        s_mmset = sem("s_mmset")
        s_ready = sem("s_ready")
        s_alone = sem("s_alone")
        xcur_in = sem("xcur_in")
        y_mm = sem("y_mm")
        y_hi_done = sem("y_hi_done")
        y_split = sem("y_split")
        yt_in = [sem("yt_in_a"), sem("yt_in_b")]
        l0_done = sem("l0_done")
        hi_done = sem("hi_done")
        split_done = sem("split_done")
        a_done = sem("a_done")
        p_copied = sem("p_copied")
        w1_done = sem("w1_done")
        q_done = sem("q_done")
        q_free = sem("q_free")
        hb_in = sem("hb_in")
        b_h = sem("b_h")
        b_dve = sem("b_dve")
        b_var = sem("b_var")
        b_root = sem("b_root")
        b_xn = sem("b_xn")
        b_xt = sem("b_xt")
        b_xtc = sem("b_xtc")
        b_s = sem("b_s")
        b_vo = sem("b_vo")
        b_sc = sem("b_sc")
        b_voc = sem("b_voc")
        b_lg = sem("b_lg")
        b_at = sem("b_at")
        b_cx = sem("b_cx")
        b_h2 = sem("b_h2")
        b_xn2 = sem("b_xn2")
        b_x2t = sem("b_x2t")
        b_x2c = sem("b_x2c")
        b_gate = sem("b_gate")
        b_top = sem("b_top")
        s_onerow = sem("s_onerow")
        c_gap = sem("c_gap")
        c_exp = sem("c_exp")
        c_dve = sem("c_dve")
        c_wd = sem("c_wd")
        z_done = sem("z_done")
        z_act = sem("z_act")
        y_done = sem("y_done")
        y_half = sem("y_half")
        d_dve = sem("d_dve")
        y_used = sem("y_used")
        o_done = sem("o_done")
        o_out = [sem("o_out_a"), sem("o_out_b")]

        block = ctx.enter_context(nc.Block())

        def alone(eng, semaphore, value):
            eng.wait_ge(semaphore, value)
            eng.sem_inc(s_alone, 1)

        names = ["g0", "beta0", "wsum", "absb", "yb", "pyb", "sx", "isx", "pra", "sa", "isa", "bound", "pb",
                 "t", "it", "wscale", "rs", "g1", "beta1", "nbeta1", "absum", "ipyb", "ipra", "ipb", "isx2", "tmp"]
        cols = {n: col[:, k:k + 1] for k, n in enumerate(names)}

        SMALL = [(ident, "ident"), (at32, "at"), (a32, "a"), (w0t, "w0t"), (bn0, "bn0"), (bn1, "bn1"), (w1, "w1")]
        LATE = [(causal, "causal"), (iota8, "iota8"), (w2, "w2"), (wq, "wq"), (wk, "wk"), (wv, "wv"), (wot, "wot"),
                (wg, "wg"), (ew1, "ew1"), (ew2, "ew2")]

        @block.sync
        def _(sp):
            for t, name in SMALL:
                sp.dma_start(t[:, :], dram[name]).then_inc(s_par, 16)
            sp.dma_start(bn1row[:, :, :], dram["bn1t"].partition_broadcast(P)).then_inc(s_par, 16)
            sp.dma_start(bn2row[:, :, :], dram["bn2t"].partition_broadcast(P)).then_inc(s_par, 16)
            per = PADDED * CIN // XLOADS
            for n in range(XLOADS):
                sp.dma_start(xs[0:V, n * per:(n + 1) * per], dram["x"][:, n * per:(n + 1) * per]).then_inc(x_in[n], 16)
            for t, name in LATE:
                if t is ew2:
                    sp.dma_start(t[:, :, :], dram[name]).then_inc(s_late, 16)
                else:
                    sp.dma_start(t[:, :], dram[name]).then_inc(s_late, 16)
            sp.dma_start(eb2[:, :], dram["eb2"].partition_broadcast(P)).then_inc(s_late, 16)

            sp.wait_ge(s_asplit, 3)
            for b in range(BLOCKS):
                for row, rows, node, frame in SPANS[b]:
                    c0 = ABASE[b] + frame * V
                    for dst, src in ((ablkhi, ahi), (ablklo, alo)):
                        sp.dma_start(dst[row:row + rows, c0:c0 + V], src[node:node + rows, :]).then_inc(s_ablk, 16)

            def load_y(half):
                for k, part in enumerate((yhi, yhi, ylo, ylo)):
                    sp.dma_start(yt[CIN * k:CIN * k + CIN, half * HALF * V:(half + 1) * HALF * V],
                                 part[half * CIN * HALF:(half + 1) * CIN * HALF, :]).then_inc(yt_in[half], 16)

            sp.wait_ge(y_split, 1)
            load_y(0)
            load_y(1)
            with sp.Fori(0, ITERS - 1) as i:
                sp.wait_ge(y_split, i + 2)
                sp.wait_ge(l0_done, i * GROUPS + GROUPS // 2)
                load_y(0)
                sp.wait_ge(l0_done, i * GROUPS + GROUPS)
                load_y(1)

            with sp.Fori(0, QUADS) as j:
                for h in range(2):
                    sp.wait_ge(o_done, 2 * j + h + 1)
                    src = ofin[:, h * 2 * D:(h + 1) * 2 * D].rearrange("p (t d) -> p t d", t=2)
                    sp.dma_start(out[bass.ds(j * QUAD + 2 * h, 2), :, :].rearrange("t p d -> p t d"), src)\
                      .then_inc(o_out[h], 16)
            sp.wait_ge(o_out[0], 16 + 16 * QUADS)
            sp.wait_ge(o_out[1], 16 + 16 * QUADS)

        @block.gpsimd
        def _(pool):
            pool.wait_ge(s_stat, 1)
            pool.partition_all_reduce(top[:, :], stat[:, :], P, bass.bass_isa.ReduceOp.max).then_inc(s_top, 1)
            pool.tensor_copy(xcur[:, :], xs[0:V, 0:XCOLS]).then_inc(xcur_in, 1)
            with pool.Fori(0, ITERS - 1) as i:
                pool.wait_ge(y_mm, i + 1)
                pool.tensor_copy(xcur[:, :], xs[0:V, bass.ds(i * XCOLS + XCOLS, XCOLS)]).then_inc(xcur_in, 1)

        @block.scalar
        def _(act):
            def y_high(i):
                act.wait_ge(y_mm, i + 1)
                act.activation(yhi[:, :], bank[6][0:XCOLS, 0:V], ACT.Copy, scale=cols["sx"][0:XCOLS, :])\
                   .then_inc(y_hi_done, 1)

            def h0_high(G, s):
                act.wait_ge(l0_done, G + 1)
                act.activation(h0hi[:, s % 2, :], bank[s % 2][0:BLOCK, 0:BLOCKS * C], ACT.Relu).then_inc(hi_done, 1)

            def p_copy(G, s):
                act.wait_ge(a_done, G + 1)
                act.activation(pt[:, s % 2, :], bank[2 + s % 2][:, 0:GROUP], ACT.Copy).then_inc(p_copied, 1)

            act.wait_ge(s_var, 1)
            act.activation(root[:, :], vareps[:, :], ACT.Sqrt).then_inc(s_root, 1)
            act.wait_ge(s_set, 1)
            y_high(0)
            h0_high(0, 0)
            h0_high(1, 1)
            p_copy(0, 0)
            h0_high(2, 2)

            def body(i, last=False):
                for s in range(GROUPS):
                    G = i * GROUPS + s
                    if not (last and s + 1 >= GROUPS):
                        act.wait_ge(w1_done, G)
                        p_copy(G + 1, s + 1)
                    if not (last and s + 3 >= GROUPS):
                        h0_high(G + 3, s + 3)
                    if s == 0 and not last:
                        act.wait_ge(yt_in[0], 64 * (i + 1))
                        act.wait_ge(yt_in[1], 64 * (i + 1))
                        y_high(i + 1)

            with act.Fori(0, ITERS - 1) as i:
                body(i)
            body(ITERS - 1, last=True)

            act.wait_ge(q_free, 2 + ITERS * GROUPS)
            with act.Fori(0, QUADS) as j:
                act.wait_ge(b_h, j)
                act.activation(hb, hbar[:, bass.ds(j * QTOK, QTOK)], ACT.Copy).then_inc(hb_in, 1)
                act.wait_ge(b_var, 2 * j + 1)
                act.activation(rstd, ve, ACT.Sqrt).then_inc(b_root, 1)
                act.wait_ge(b_xt, j + 1)
                act.activation(xnt, bank[1][0:D, :], ACT.Copy).then_inc(b_xtc, 1)
                act.wait_ge(b_s, j + 1)
                act.activation(st, bank[2][0:D, :], ACT.Copy).then_inc(b_sc, 1)
                act.wait_ge(b_var, 2 * j + 2)
                act.activation(rstd, ve, ACT.Sqrt).then_inc(b_root, 1)
                act.wait_ge(b_x2t, j + 1)
                act.wait_ge(b_gate, j)
                act.wait_ge(s_onerow, 1)
                act.activation(xn2q[0:D, :], bank[6][0:D, :], ACT.Copy).then_inc(b_x2c, 1)
                act.activation(xn2t[0:D, bass.ds(j * QTOK, QTOK)], bank[6][0:D, :], ACT.Copy).then_inc(b_x2c, 1)

            act.wait_ge(c_gap, 1)
            act.activation(egap, gap, ACT.Exp).then_inc(c_exp, 1)

            with act.Fori(0, QUADS) as j:
                for h in range(2):
                    for e in range(2 * E):
                        n = (2 * j + h) * 2 * E + e
                        act.wait_ge(z_done, n + 1)
                        if True:
                            act.wait_ge(y_half, n)
                        act.activation(gelu[:, (e % 2) * QTOK:(e % 2) * QTOK + PAIR], bank[e % 2][:, 0:PAIR], ACT.Gelu)\
                           .then_inc(z_act, 1)

        @block.vector
        def _(v):
            links = [0]

            def link(ins):
                links[0] += 1
                ins.then_inc(s_chain, 1)
                v.wait_ge(s_chain, links[0])

            c = cols
            v.memset(ones[:, :], 1.0).then_inc(s_ones, 1)
            v.memset(ablkhi[:, :], 0.0).then_inc(s_asplit, 1)
            v.memset(ablklo[:, :], 0.0).then_inc(s_asplit, 1)
            v.sem_inc(q_done, 2)
            v.sem_inc(q_free, 2)
            v.sem_inc(y_used, 2)
            v.sem_inc(o_out[0], 16)
            v.sem_inc(o_out[1], 16)
            link(v.memset(yt[:, :], 1.0))
            link(v.memset(stat[:, :], 0.0))
            v.wait_ge(s_par, 16 * (len(SMALL) + 2))
            link(v.tensor_copy(ident16[:, :], ident[:, :]))
            link(v.tensor_reduce(stat[0:V, 1:2], a32[:, :], X, ALU.add, apply_absolute_value=True))

            for k, var in ((0, bn0[:, 4:5]), (1, bn1[:, 4:5])):
                link(v.tensor_scalar(vareps[:, k:k + 1], var, EPS, None, ALU.add))
            link(v.tensor_scalar(vareps[:, 2:2 + C], bn1row[:, 4, :], EPS, None, ALU.add))
            v.tensor_scalar(vareps[:, 2 + C:], bn2row[:, 4, :], EPS, None, ALU.add).then_inc(s_var, 1)
            v.wait_ge(s_root, 1)
            link(v.reciprocal(root[:, :], root[:, :]))
            link(v.scalar_tensor_tensor(newton[:, :], root[:, :], -0.5, root[:, :], ALU.mult, ALU.mult))
            link(v.tensor_tensor(newton[:, :], newton[:, :], vareps[:, :], ALU.mult))
            link(v.scalar_tensor_tensor(root[:, :], newton[:, :], 1.5, root[:, :], ALU.add, ALU.mult))

            def batchnorm(b, inverse, gain, beta):
                link(v.tensor_tensor(gain, inverse, b[1], ALU.mult))
                if beta is not None:
                    link(v.tensor_tensor(beta, b[0], b[3], ALU.subtract))
                    link(v.tensor_tensor(beta, beta, gain, ALU.mult))
                    link(v.tensor_tensor(beta, beta, b[2], ALU.add))

            batchnorm([bn0[:, k:k + 1] for k in range(5)], root[:, 0:1], c["g0"], c["beta0"])
            batchnorm([bn1[:, k:k + 1] for k in range(5)], root[:, 1:2], c["g1"], c["beta1"])
            batchnorm([bn1row[:, k, :] for k in range(5)], root[:, 2:2 + C], g1row[:, :], None)
            batchnorm([bn2row[:, k, :] for k in range(5)], root[:, 2 + C:], g2row[:, :], bias2[:, :])
            link(v.tensor_scalar(c["nbeta1"], c["beta1"], -1.0, None, ALU.mult))
            link(v.tensor_scalar(w4[:, 0:CIN], w0t[:, :], c["g0"], None, ALU.mult))
            link(v.tensor_reduce(c["wsum"], w4[:, 0:CIN], X, ALU.add, apply_absolute_value=True))
            link(v.tensor_reduce(c["absb"], c["beta0"], X, ALU.add, apply_absolute_value=True))
            per = PADDED * CIN // XLOADS
            for n in range(XLOADS):
                v.wait_ge(x_in[n], 16)
                link(v.tensor_reduce(xmax[0:V, n:n + 1], xs[0:V, n * per:(n + 1) * per], X, ALU.max,
                                     apply_absolute_value=True))
            v.tensor_reduce(stat[0:V, 0:1], xmax[0:V, :], X, ALU.max).then_inc(s_stat, 1)
            v.wait_ge(s_top, 1)

            def power_of_two(dst, src):
                link(v.tensor_scalar(dst, src, TINY, None, ALU.max))
                link(v.tensor_single_scalar(dst.bitcast(U32), dst.bitcast(U32), 0x7F800000, ALU.bitwise_and))

            power_of_two(c["pra"], top[:, 1:2])
            link(v.reciprocal(c["ipra"], c["pra"]))
            link(v.tensor_scalar(c["sa"], c["ipra"], ATOP, None, ALU.mult))
            link(v.tensor_scalar(ascaled[:, :], at32[:, :], c["sa"][0:V, :], None, ALU.mult))
            link(v.tensor_copy(ahi[:, :], ascaled[:, :]))
            v.tensor_tensor(alo[:, :], ascaled[:, :], ahi[:, :], ALU.subtract).then_inc(s_asplit, 1)
            link(v.tensor_tensor(c["yb"], top[:, 0:1], top[:, 1:2], ALU.mult))
            link(v.tensor_scalar(c["yb"], c["yb"], SLACK, None, ALU.mult))
            power_of_two(c["pyb"], c["yb"])
            link(v.reciprocal(c["ipyb"], c["pyb"]))
            link(v.tensor_scalar(c["sx"], c["ipyb"], YTOP, None, ALU.mult))
            link(v.tensor_scalar(c["isx"], c["pyb"], 1.0 / YTOP, None, ALU.mult))
            link(v.scalar_tensor_tensor(c["bound"], c["wsum"], c["yb"], c["absb"], ALU.mult, ALU.add))
            link(v.tensor_scalar(c["bound"], c["bound"], SLACK, None, ALU.mult))
            power_of_two(c["pb"], c["bound"])
            link(v.reciprocal(c["ipb"], c["pb"]))
            link(v.tensor_scalar(c["t"], c["ipb"], HTOP, None, ALU.mult))
            link(v.tensor_tensor(c["wscale"], c["t"], c["isx"], ALU.mult))
            link(v.tensor_scalar(w4[:, 0:CIN], w4[:, 0:CIN], c["wscale"], None, ALU.mult))
            link(v.tensor_tensor(w4[:, 3:4], c["beta0"], c["t"], ALU.mult))
            link(v.tensor_copy(w4hi[:, :], w4[:, :]))
            link(v.tensor_tensor(w4lo[:, :], w4[:, :], w4hi[:, :], ALU.subtract))
            for k, part in enumerate((w4hi, w4lo, w4hi, w4lo)):
                link(v.tensor_copy(w0cols[:, CIN * k:CIN * k + CIN], part[:, 0:CIN]))
            link(v.tensor_copy(w0cols[:, 12:13], w4hi[:, 3:4]))
            v.tensor_copy(w0cols[:, 13:14], w4lo[:, 3:4]).then_inc(s_w0c, 1)
            link(v.tensor_scalar(c["it"], c["pb"], 1.0 / HTOP, None, ALU.mult))
            link(v.tensor_scalar(c["isa"], c["pra"], 1.0 / ATOP, None, ALU.mult))
            link(v.tensor_tensor(c["rs"], c["it"], c["isa"], ALU.mult))
            link(v.scalar_tensor_tensor(w1s[:, :], w1[:, :], c["rs"], g1row[:, :], ALU.mult, ALU.mult))
            v.wait_ge(s_w0t, 1)
            v.tensor_copy(w0x[:, :], bank[7][0:YROWS, 0:C // 2].bitcast(F16)).then_inc(s_w0x, 1)
            v.wait_ge(s_abar, 1)
            for k in range(FRAMES):
                link(v.tensor_scalar(abar[:, k, :], bank[5][:, 0:V], 1.0 / V, None, ALU.mult))
            v.sem_inc(s_set, 1)

            def y_low(i):
                v.wait_ge(y_hi_done, i + 1)
                v.scalar_tensor_tensor(ylo[:, :], bank[6][0:XCOLS, 0:V], c["sx"][0:XCOLS, :], yhi[:, :],
                                       ALU.mult, ALU.subtract).then_inc(y_split, 1)

            def h0_low(G, s):
                v.wait_ge(hi_done, G + 1)
                v.scalar_tensor_tensor(h0lo[:, s % 2, :], bank[s % 2][0:BLOCK, 0:BLOCKS * C], 0.0, h0hi[:, s % 2, :],
                                       ALU.max, ALU.subtract).then_inc(split_done, 1)

            y_low(0)
            h0_low(0, 0)
            h0_low(1, 1)
            h0_low(2, 2)

            def body(i, last=False):
                for s in range(GROUPS):
                    G = i * GROUPS + s
                    v.wait_ge(w1_done, G + 1)
                    v.wait_ge(q_free, G + 1)
                    v.scalar_tensor_tensor(q[:, s % 2, :], bank[4 + s % 2][:, 0:GROUP], c["nbeta1"],
                                           abar[:, :, :].rearrange("p f u -> p (f u)"), ALU.max, ALU.mult)\
                     .then_inc(q_done, 1)
                    if not (last and s + 3 >= GROUPS):
                        h0_low(G + 3, s + 3)
                    v.wait_ge(q_done, G + 3)
                    v.tensor_reduce(hbar[:, bass.ds(i * STEP + s * FRAMES, FRAMES)],
                                    q[:, s % 2, :].rearrange("p (f u) -> p f u", u=V), X, ALU.add).then_inc(q_free, 1)
                    if s == 0 and not last:
                        y_low(i + 1)

            with v.Fori(0, ITERS - 1) as i:
                body(i)
            body(ITERS - 1, last=True)

            v.wait_ge(s_late, 16 * (len(LATE) + 1))
            link(v.tensor_tensor(w2s[:, :], w2[:, :], g2row[:, :], ALU.mult))
            link(v.tensor_reduce(c["absum"], abar[:, 0, :], X, ALU.add))
            link(v.tensor_tensor(c["tmp"], c["absum"], c["beta1"], ALU.mult))
            v.tensor_scalar(corr[:, :], ones[:, :], c["tmp"], None, ALU.mult).then_inc(s_corr, 1)
            v.wait_ge(s_mmset, 1)
            link(v.tensor_tensor(bias2[:, :], bias2[:, :], bank[7][:, 0:D], ALU.add))
            link(v.tensor_copy(mqk[:, :], bank[7][0:D, D:2 * D]))
            link(v.tensor_copy(nvo[:, :], bank[7][0:D, 2 * D:3 * D]))
            v.sem_inc(s_ready, 1)
            v.memset(xn2q[D:D + 1, :], 1.0).then_inc(s_onerow, 1)
            v.wait_ge(q_free, 2 + ITERS * GROUPS)
            v.memset(xn2t[D:D + 1, :], 1.0).then_inc(s_onerow, 1)
            v.wait_ge(s_onerow, 2)

            def norm(j, which_norm, base, k, dst, src):
                for t in range(QUAD):
                    v.bn_stats(bn[:, 6 * t:6 * t + 6], src[:, t * D:(t + 1) * D]).then_inc(b_dve, 1)
                alone(v, b_dve, base + k + QUAD)
                for t in range(QUAD):
                    v.bn_aggr(mv[:, 2 * t:2 * t + 2], bn[:, 6 * t:6 * t + 6]).then_inc(b_dve, 1)
                v.wait_ge(b_dve, base + k + 2 * QUAD)
                v.tensor_scalar(ve, mv.rearrange("p (t s) -> p t s", s=2)[:, :, 1], EPS, None, ALU.add).then_inc(b_var, 1)
                v.wait_ge(b_root, 2 * j + which_norm + 1)
                v.reciprocal(rstd, rstd).then_inc(b_dve, 1)
                k += 2 * QUAD + 1
                v.wait_ge(b_dve, base + k)
                v.scalar_tensor_tensor(nt, rstd, -0.5, rstd, ALU.mult, ALU.mult).then_inc(b_dve, 1)
                k += 1
                v.wait_ge(b_dve, base + k)
                v.tensor_tensor(nt, nt, ve, ALU.mult).then_inc(b_dve, 1)
                k += 1
                v.wait_ge(b_dve, base + k)
                v.scalar_tensor_tensor(rstd, nt, 1.5, rstd, ALU.add, ALU.mult).then_inc(b_dve, 1)
                k += 1
                v.wait_ge(b_dve, base + k)
                for t in range(QUAD):
                    last = v.tensor_scalar(dst[:, t * D:(t + 1) * D], src[:, t * D:(t + 1) * D], mv[:, 2 * t:2 * t + 1],
                                           rstd[:, t:t + 1], ALU.subtract, ALU.mult)
                    if t < QUAD - 1:
                        last.then_inc(b_dve, 1)
                return last, k + QUAD - 1

            STEPS = 1 + 2 * (3 * QUAD + 3) + 1 + 1 + 2 * QUAD
            with v.Fori(0, QUADS) as j:
                base = j * STEPS
                v.wait_ge(b_h, j + 1)
                v.tensor_tensor(hs.rearrange("p (t d) -> p t d", t=QUAD),
                                bank[0][:, 0:QUAD * D].rearrange("p (t d) -> p t d", t=QUAD),
                                bias2[:, :].unsqueeze(1).broadcast_to([P, QUAD, D]), ALU.add).then_inc(b_dve, 1)
                v.wait_ge(b_dve, base + 1)
                last, k = norm(j, 0, base, 1, xn, hs)
                last.then_inc(b_xn, 1)
                v.wait_ge(b_vo, j + 1)
                v.tensor_copy(vo, bank[3][:, 0:QUAD * D]).then_inc(b_voc, 1)
                v.wait_ge(b_lg, j + 1)
                v.scalar_tensor_tensor(attn.rearrange("p (t l) -> p t l", t=QUAD),
                                       bank[4][:, :].rearrange("p (t l) -> p t l", t=QUAD), 0.0,
                                       causal[:, :].unsqueeze(1).broadcast_to([P, QUAD, TILE]), ALU.max, ALU.mult)\
                 .then_inc(b_at, 1)
                v.wait_ge(b_cx, j + 1)
                v.tensor_tensor(h2, hs, bank[5][:, 0:QUAD * D], ALU.add).then_inc(b_dve, 1)
                k += 1
                v.wait_ge(b_dve, base + k)
                v.tensor_copy(h2all[:, bass.ds(j * QUAD * D, QUAD * D)], h2).then_inc(b_h2, 1)
                last, k = norm(j, 1, base, k, xn2, h2)
                last.then_inc(b_xn2, 1)
                v.wait_ge(b_gate, j + 1)
                v.tensor_copy(gl, bank[7][:, 0:QUAD * E]).then_inc(b_dve, 1)
                k += 1
                alone(v, b_dve, base + k)
                for t in range(QUAD):
                    v.max(mx[:, 8 * t:8 * t + 8], gl[:, E * t:E * t + E]).then_inc(b_dve, 1)
                    k += 1
                alone(v, b_dve, base + k)
                for t in range(QUAD):
                    v.max_index(mi[:, 8 * t:8 * t + 8], mx[:, 8 * t:8 * t + 8], gl[:, E * t:E * t + E]).then_inc(b_dve, 1)
                    k += 1
                v.wait_ge(b_dve, base + k)
                first = lambda a: a.rearrange("p (t k) -> p t k", k=8)[:, :, 0:2]
                v.tensor_copy(best[:, bass.ds(j * QUAD * 2, QUAD * 2)].rearrange("p (t k) -> p t k", k=2), first(mx))\
                 .then_inc(b_top, 1)
                v.tensor_copy(which[:, bass.ds(j * QUAD * 2, QUAD * 2)].rearrange("p (t k) -> p t k", k=2), first(mi))\
                 .then_inc(b_top, 1)
                v.wait_ge(b_top, 2 * j + 2)
                v.wait_ge(b_h2, j + 1)
                assert k == STEPS

            n = [0]

            def step(ins):
                n[0] += 1
                ins.then_inc(c_dve, 1)
                v.wait_ge(c_dve, n[0])

            pair = best.rearrange("p (t k) -> p t k", k=2)
            v.tensor_tensor(gap, pair[:, :, 1], pair[:, :, 0], ALU.subtract).then_inc(c_gap, 1)
            v.wait_ge(c_exp, 1)
            step(v.tensor_scalar(den, egap, 1.0, None, ALU.add))
            step(v.reciprocal(prob[:, 0:TILES], den))
            step(v.tensor_tensor(prob[:, TILES:2 * TILES], prob[:, 0:TILES], egap, ALU.mult))
            wd3 = wd.rearrange("p (t e) -> p t e", e=E)
            hit3 = hit.rearrange("p (t e) -> p t e", e=E)
            expert = iota8[:, :].unsqueeze(1).broadcast_to([P, TILES, E])
            chosen = which.rearrange("p (t k) -> p t k", k=2)
            for k, dst in enumerate((wd3, hit3)):
                step(v.tensor_tensor(dst, expert, chosen[:, :, k:k + 1].broadcast_to([P, TILES, E]), ALU.is_equal))
                step(v.tensor_tensor(dst, dst, prob[:, k * TILES:(k + 1) * TILES].unsqueeze(2)
                                     .broadcast_to([P, TILES, E]), ALU.mult))
            step(v.tensor_tensor(wd, wd, hit, ALU.add))
            v.sem_inc(c_wd, 1)

            with v.Fori(0, QUADS) as j:
                for h in range(2):
                    v.wait_ge(y_half, (2 * j + h + 1) * 2 * E)
                    v.wait_ge(o_out[h], 16 * j + 16)
                    for t in range(2):
                        k = 2 * h + t
                        tile_no = j * QUAD + k
                        yc = ycomb[:, t * E * D:(t + 1) * E * D]
                        base = 16 * j + 4 * k
                        ins = v.tensor_tensor(yc, bank[2 + k][:, :], eb2[:, :], ALU.add)
                        ins.then_inc(y_used if t == 1 else d_dve, 1) if False else ins.then_inc(d_dve, 1)
                        v.wait_ge(d_dve, base + 1)
                        if t == 1:
                            v.sem_inc(y_used, 1)
                        v.tensor_tensor(yc.rearrange("p (e d) -> p e d", e=E), yc.rearrange("p (e d) -> p e d", e=E),
                                        wd[:, bass.ds(tile_no * E, E)].unsqueeze(2).broadcast_to([P, E, D]), ALU.mult)\
                         .then_inc(d_dve, 1)
                        v.wait_ge(d_dve, base + 2)
                        v.tensor_reduce(osum[:, k * D:(k + 1) * D], yc.rearrange("p (e d) -> p d e", e=E), X, ALU.add)\
                         .then_inc(d_dve, 1)
                        v.wait_ge(d_dve, base + 3)
                        v.tensor_tensor(ofin[:, k * D:(k + 1) * D], osum[:, k * D:(k + 1) * D],
                                        h2all[:, bass.ds(tile_no * D, D)], ALU.add).then_inc(d_dve, 1)
                        v.wait_ge(d_dve, base + 4)
                    v.sem_inc(o_done, 1)

        @block.tensor
        def _(pe):
            def y_product(i):
                pe.wait_ge(xcur_in, i + 1)
                pe.matmul(bank[6][0:XCOLS, 0:V], xcur[:, :], at32[:, :], start=True, stop=True).then_inc(y_mm, 1)

            def l0(s):
                g = s % GROUPS
                for b in range(BLOCKS):
                    n = (g * BLOCKS + b) * BLOCK
                    mm = pe.matmul(bank[s % 2][0:BLOCK, b * C:(b + 1) * C], yt[:, n:n + BLOCK], w0x[:, :],
                                   start=True, stop=True, skip_group_check=True)
                mm.then_inc(l0_done, 1)

            def a_product(s):
                first = True
                for b in range(BLOCKS):
                    width = len(SPANS[b]) * V
                    c0 = FIRST_FRAME[b] * V
                    for h, a in ((h0hi, ablkhi), (h0hi, ablklo), (h0lo, ablkhi)):
                        mm = pe.matmul(bank[2 + s % 2][:, c0:c0 + width], h[:, s % 2, b * C:(b + 1) * C],
                                       a[0:BLOCK, ABASE[b]:ABASE[b] + width], start=first,
                                       stop=(b == BLOCKS - 1 and h is h0lo), skip_group_check=True)
                        first = False
                mm.then_inc(a_done, 1)

            def w1_product(s):
                pe.matmul(bank[4 + s % 2][:, 0:GROUP], w1s[:, :], pt[:, s % 2, :], start=True, stop=True)\
                  .then_inc(w1_done, 1)

            pe.wait_ge(s_ones, 1)
            pe.wait_ge(s_par, 16 * (len(SMALL) + 2))
            pe.matmul(bank[5][:, 0:V], ones[0:V, :], a32[:, :], start=True, stop=True).then_inc(s_abar, 1)
            pe.wait_ge(s_w0c, 1)
            pe.transpose(bank[7][0:YROWS, 0:C // 2].bitcast(F16), w0cols[:, :], ident16[:, :]).then_inc(s_w0t, 1)
            pe.wait_ge(s_w0x, 1)
            y_product(0)
            pe.wait_ge(s_ablk, 16 * 2 * sum(len(x) for x in SPANS))
            pe.wait_ge(s_set, 1)
            pe.wait_ge(yt_in[0], 64)
            l0(0)
            l0(1)
            pe.wait_ge(split_done, 1)
            a_product(0)
            l0(2)

            def body(i, last=False):
                for s in range(GROUPS):
                    G = i * GROUPS + s
                    if not (last and s + 1 >= GROUPS):
                        pe.wait_ge(split_done, G + 2)
                        a_product(s + 1)
                    if s == 1:
                        pe.wait_ge(yt_in[1], 64 * (i + 1))
                    if s == 5 and not last:
                        pe.wait_ge(yt_in[0], 64 * (i + 2))
                    if not (last and s + 3 >= GROUPS):
                        l0(s + 3)
                    if s == 0 and not last:
                        y_product(i + 1)
                    pe.wait_ge(p_copied, G + 1)
                    pe.wait_ge(q_done, G + 1)
                    w1_product(s)

            with pe.Fori(0, ITERS - 1) as i:
                body(i)
            body(ITERS - 1, last=True)

            pe.wait_ge(s_corr, 1)
            pe.matmul(bank[7][:, 0:D], corr[:, :], w2s[:, :], start=True, stop=True, skip_group_check=True)
            pe.matmul(bank[7][0:D, D:2 * D], wq[:, :], wk[:, :], start=True, stop=True, skip_group_check=True)
            pe.matmul(bank[7][0:D, 2 * D:3 * D], wv[:, :], wot[:, :], start=True, stop=True, skip_group_check=True)\
              .then_inc(s_mmset, 1)
            pe.wait_ge(s_ready, 1)

            tok = lambda t: slice(t * TILE, (t + 1) * TILE)
            ch = lambda t: slice(t * D, (t + 1) * D)
            with pe.Fori(0, QUADS) as j:
                pe.wait_ge(hb_in, j + 1)
                for t in range(QUAD):
                    mm = pe.matmul(bank[0][:, ch(t)], hb[:, tok(t)], w2s[:, :], start=True, stop=True)
                mm.then_inc(b_h, 1)
                alone(pe, b_xn, j + 1)
                for t in range(QUAD):
                    mm = pe.transpose(bank[1][0:D, tok(t)], xn[:, ch(t)], ident[:, :])
                mm.then_inc(b_xt, 1)
                alone(pe, b_xtc, j + 1)
                pe.matmul(bank[2][0:D, :], mqk[:, :], xnt, start=True, stop=True).then_inc(b_s, 1)
                for t in range(QUAD):
                    mm = pe.matmul(bank[3][:, ch(t)], xnt[:, tok(t)], nvo[:, :], start=True, stop=True)
                mm.then_inc(b_vo, 1)
                pe.wait_ge(b_sc, j + 1)
                for t in range(QUAD):
                    mm = pe.matmul(bank[4][:, tok(t)], xnt[:, tok(t)], st[:, tok(t)], start=True, stop=True)
                mm.then_inc(b_lg, 1)
                pe.wait_ge(b_voc, j + 1)
                pe.wait_ge(b_at, j + 1)
                for t in range(QUAD):
                    mm = pe.matmul(bank[5][:, ch(t)], attn[:, tok(t)], vo[:, ch(t)], start=True, stop=True)
                mm.then_inc(b_cx, 1)
                alone(pe, b_xn2, j + 1)
                for t in range(QUAD):
                    mm = pe.transpose(bank[6][0:D, tok(t)], xn2[:, ch(t)], ident[:, :])
                mm.then_inc(b_x2t, 1)
                pe.wait_ge(b_x2c, 2 * j + 2)
                for t in range(QUAD):
                    mm = pe.matmul(bank[7][:, t * E:(t + 1) * E], xn2q[:, tok(t)], wg[:, :], start=True, stop=True)
                mm.then_inc(b_gate, 1)

            pe.wait_ge(b_top, 2 * QUADS)
            pe.wait_ge(c_wd, 1)
            with pe.Fori(0, QUADS) as j:
                for h in range(2):
                    def z_product(e):
                        pe.matmul(bank[e % 2][:, 0:PAIR], ew1[:, e * P:(e + 1) * P],
                                  xn2t[:, bass.ds(j * QTOK + h * PAIR, PAIR)], start=True, stop=True).then_inc(z_done, 1)

                    n0 = (2 * j + h) * 2 * E
                    z_product(0)
                    for e in range(2 * E):
                        if e + 1 < 2 * E:
                            if e > 0:
                                pe.wait_ge(z_act, n0 + e)
                            z_product(e + 1)
                        pe.wait_ge(z_act, n0 + e + 1)
                        if e == 0:
                            pe.wait_ge(y_used, 2 * j + h + 1)
                        for t in range(2):
                            mm = pe.matmul(bank[2 + 2 * h + t][:, (e // 2) * D:(e // 2 + 1) * D],
                                           gelu[:, (e % 2) * QTOK + t * TILE:(e % 2) * QTOK + (t + 1) * TILE],
                                           ew2[:, e, :], start=(e % 2 == 0), stop=(e % 2 == 1))
                        mm.then_inc(y_half, 1)
                        if e == 2 * E - 1:
                            pass



def kernel(**inputs):
    import numpy as _np
    import concourse.bacc as _bacc
    from concourse.bass_utils import run_bass_kernel_spmd as _run

    g = {k: _np.ascontiguousarray(v) for k, v in inputs.items()}
    x = _np.zeros((PADDED, V, CIN), _np.float32)
    x[:TOKENS] = g["x"].reshape(TOKENS, V, CIN)
    bn = [_np.stack([g[f"L0_tok_{n}{i}"] for n in ("b", "g", "be", "m", "v")]) for i in range(3)]
    token = _np.arange(TILE)
    allowed = (token[:, None] <= token[None, :]) & (token[:, None] // T == token[None, :] // T)
    arrays = {
        "x": x.reshape(2 * ITERS, HALF, V, CIN).transpose(2, 0, 3, 1).reshape(V, PADDED * CIN),
        "a": g["L0_tok_A"], "at": g["L0_tok_A"].T,
        "w0t": g["L0_tok_W0"].T, "w1": g["L0_tok_W1"], "w2": g["L0_tok_W2"],
        "bn0": bn[0].T, "bn1": bn[1].T, "bn1t": bn[1], "bn2t": bn[2],
        "wq": g["L0_attn_Wq"], "wk": g["L0_attn_Wk"], "wv": g["L0_attn_Wv"], "wot": g["L0_attn_Wo"].T,
        "wg": _np.concatenate([g["L0_ffn_Wg"], g["L0_ffn_bg"][None]]),
        "ew1": _np.concatenate([g["L0_ffn_W1"], g["L0_ffn_b1"][:, None]], 1).transpose(1, 0, 2).reshape(D + 1, E * H),
        "ew2": g["L0_ffn_W2"].reshape(2 * E, P, D).transpose(1, 0, 2),
        "eb2": g["L0_ffn_b2"].reshape(E * D),
        "ident": _np.eye(P, dtype=_np.float32),
        "causal": (allowed / _np.maximum(token % T, 1)[None, :]).astype(_np.float32),
        "iota8": _np.tile(_np.arange(E, dtype=_np.float32), (P, 1)),
    }
    arrays = {f"in_{k}": _np.ascontiguousarray(v) for k, v in arrays.items()}
    nc = _bacc.Bacc("TRN2", target_bir_lowering=False, num_devices=1)
    dram = {k[3:]: nc.dram_tensor(k, v.shape, F32, kind="ExternalInput").ap() for k, v in arrays.items()}
    out = nc.dram_tensor("out_0", (TILES, TILE, D), F32, kind="ExternalOutput").ap()
    build(nc, dram, out)
    r = _run(nc, [arrays], core_ids=[0])
    return r.results[0]["out_0"].reshape(B, T, D)
```

```python
from contextlib import ExitStack

import numpy as np

import concourse.bass as bass
from concourse import mybir

F32 = mybir.dt.float32
F16 = mybir.dt.float16
U32 = mybir.dt.uint32
ALU = mybir.AluOpType
ACT = mybir.ActivationFunctionType
X = mybir.AxisListType.X

P = 128
EPS = 1e-5
B, T, V, CIN = 128, 64, 75, 3
C = 128
D = 64
E, H = 8, 256
TOKENS = B * T

FRAMES = 5
BLOCK = 125
BLOCKS = FRAMES * V // BLOCK
GROUP = FRAMES * V
GROUPS = 8
HALF = GROUPS // 2 * FRAMES
STEP = 2 * HALF
ITERS = -(-TOKENS // STEP)
PADDED = ITERS * STEP
XCOLS = 2 * CIN * HALF
XLOADS = 10
YROWS = 4 * CIN + 2
SPANS = [[(0, 75, 0, 0), (75, 50, 0, 1)],
         [(0, 25, 50, 0), (25, 75, 0, 1), (100, 25, 0, 2)],
         [(0, 50, 25, 0), (50, 75, 0, 1)]]
FIRST_FRAME = [0, 1, 3]
ABASE = [0, 2 * V, 5 * V]
ACOLS = 7 * V
YTOP, HTOP, ATOP = 2.0 ** 8, 2.0 ** 14, 2.0 ** 14
TINY = 2.0 ** -60
SLACK = 1.001

TILE = 128
QUAD = 4
QTOK = QUAD * TILE
QUADS = TOKENS // QTOK
TILES = TOKENS // TILE
CHUNKS = 2 * E
SPARE = 4
XTOP = 2.0 ** 10


def build(nc, dram, out):
    ctx = ExitStack()
    with ctx:
        def sb(name, shape, dt=F32):
            return ctx.enter_context(nc.sbuf_tensor(name, shape, dt))

        def sem(name):
            return ctx.enter_context(nc.semaphore(name))

        bank = [ctx.enter_context(nc.psum_tensor(f"bank{n}", [P, 512], F32)) for n in range(8)]

        xs = sb("xs", [P, PADDED * CIN])
        hbar = sb("hbar", [P, PADDED])
        ident = sb("ident", [P, P])
        ident16 = sb("ident16", [P, P], F16)
        causal = sb("causal", [P, P])
        iota8 = sb("iota8", [P, E])
        at32 = sb("at32", [V, V])
        a32 = sb("a32", [V, V])
        w0t = sb("w0t", [P, CIN])
        bn0 = sb("bn0", [P, 5])
        bn1 = sb("bn1", [P, 5])
        bn1row = sb("bn1row", [P, 5, C])
        bn2row = sb("bn2row", [P, 5, D])
        w1 = sb("w1", [P, C])
        w2 = sb("w2", [P, D])
        wq = sb("wq", [D, D])
        wk = sb("wk", [D, D])
        wv = sb("wv", [D, D])
        wot = sb("wot", [D, D])
        wg = sb("wg", [D + 1, E])
        ew1 = sb("ew1", [P, E * H])
        eb1 = sb("eb1", [P, CHUNKS])
        ew2 = sb("ew2", [P, CHUNKS * D])
        eb2 = sb("eb2", [E * E, E * D])
        stat = sb("stat", [P, 2])
        top = sb("top", [P, 2])
        wstat = sb("wstat", [P, 3])
        wtop = sb("wtop", [P, 3])
        xmax = sb("xmax", [P, XLOADS])
        col = sb("col", [P, 40])
        w4 = sb("w4", [P, 4])
        w4hi = sb("w4hi", [P, 4], F16)
        w4lo = sb("w4lo", [P, 4], F16)
        w0cols = sb("w0cols", [P, YROWS], F16)
        w0x = sb("w0x", [YROWS, C], F16)
        ascaled = sb("ascaled", [V, V])
        ahi = sb("ahi", [V, V], F16)
        alo = sb("alo", [V, V], F16)
        ablkhi = sb("ablkhi", [P, ACOLS], F16)
        ablklo = sb("ablklo", [P, ACOLS], F16)
        vareps = sb("vareps", [P, 2 + C + D])
        root = sb("root", [P, 2 + C + D])
        newton = sb("newton", [P, 2 + C + D])
        g1row = sb("g1row", [P, C])
        w1s = sb("w1s", [P, C])
        g2row = sb("g2row", [P, D])
        w2s = sb("w2s", [P, D])
        ones = sb("ones", [P, P])
        abar = sb("abar", [P, FRAMES, V])
        corr = sb("corr", [P, P])
        bias2 = sb("bias2", [P, D])
        mqk = sb("mqk", [D, D])
        nvo = sb("nvo", [D, D])
        xcur = sb("xcur", [V, XCOLS])
        yhi = sb("yhi", [XCOLS, V], F16)
        ylo = sb("ylo", [XCOLS, V], F16)
        yt = sb("yt", [YROWS, STEP * V], F16)
        h0hi = sb("h0hi", [BLOCK, 2, BLOCKS * C], F16)
        h0lo = sb("h0lo", [BLOCK, 2, BLOCKS * C], F16)
        pt = sb("pt", [P, 2, GROUP])
        q = sb("q", [P, 2, GROUP])

        at = 0

        def again(cols, rows=P):
            nonlocal at
            view = xs[0:rows, at:at + cols]
            at += cols
            return view

        h2all = again(TILES * D)
        xn2t = again(TOKENS // 2).bitcast(F16)
        hb = again(QTOK)
        hs = again(QUAD * D)
        bn = again(QUAD * 6)
        mv = again(QUAD * 2)
        ve = again(QUAD)
        rstd = again(QUAD)
        nt = again(QUAD)
        xn = again(QUAD * D)
        xnt = again(QTOK, D)
        st = again(QTOK, D)
        vo = again(QUAD * D)
        attn = again(QTOK)
        h2 = again(QUAD * D)
        xn2 = again(QUAD * 2 * D)
        xn2q = again(QTOK, D + 1)
        gl = again(QUAD * E)
        mx = again(QUAD * 8)
        mi = again(QUAD * 8).bitcast(U32)
        best = again(TILES * 2)
        which = again(TILES * 2)
        gap = again(TILES)
        egap = again(TILES)
        prob = again(2 * TILES)
        den = again(TILES)
        hit = again(TILES * E)
        wd = again(TILES * E)
        wds = again(TILES * E)
        w1hi = again(E * H // 2).bitcast(F16)
        w1lo = again(E * H // 2).bitcast(F16)
        w2hi = again(CHUNKS * D // 2).bitcast(F16)
        w2lo = again(CHUNKS * D // 2).bitcast(F16)
        wdt = again(2 * TILE, E * E)
        gelu = again(SPARE * QTOK)
        ghi = again(SPARE * QTOK // 2).bitcast(F16)
        glo = again(SPARE * QTOK // 2).bitcast(F16)
        ycomb = again(QUAD * E * D)
        osum = again(QUAD * D)
        ofin = again(QUAD * D)
        assert at <= PADDED * CIN

        s_par = sem("s_par")
        s_late = sem("s_late")
        x_in = [sem(f"x_in{n}") for n in range(XLOADS)]
        s_chain = sem("s_chain")
        s_stat = sem("s_stat")
        s_top = sem("s_top")
        s_asplit = sem("s_asplit")
        s_ablk = sem("s_ablk")
        s_w0c = sem("s_w0c")
        s_w0t = sem("s_w0t")
        s_w0x = sem("s_w0x")
        s_ones = sem("s_ones")
        s_abar = sem("s_abar")
        s_set = sem("s_set")
        s_var = sem("s_var")
        s_root = sem("s_root")
        s_corr = sem("s_corr")
        s_mmset = sem("s_mmset")
        s_ready = sem("s_ready")
        s_alone = sem("s_alone")
        xcur_in = sem("xcur_in")
        y_mm = sem("y_mm")
        y_hi_done = sem("y_hi_done")
        y_split = sem("y_split")
        yt_in = [sem("yt_in_a"), sem("yt_in_b")]
        l0_done = sem("l0_done")
        hi_done = sem("hi_done")
        split_done = sem("split_done")
        a_done = sem("a_done")
        p_copied = sem("p_copied")
        w1_done = sem("w1_done")
        q_done = sem("q_done")
        q_free = sem("q_free")
        hb_in = sem("hb_in")
        b_h = sem("b_h")
        b_dve = sem("b_dve")
        b_var = sem("b_var")
        b_root = sem("b_root")
        b_xn = sem("b_xn")
        b_xt = sem("b_xt")
        b_xtc = sem("b_xtc")
        b_s = sem("b_s")
        b_vo = sem("b_vo")
        b_sc = sem("b_sc")
        b_voc = sem("b_voc")
        b_lg = sem("b_lg")
        b_at = sem("b_at")
        b_cx = sem("b_cx")
        b_h2 = sem("b_h2")
        b_xn2 = sem("b_xn2")
        b_x2t = sem("b_x2t")
        b_x2c = sem("b_x2c")
        b_x2h = sem("b_x2h")
        b_x2l = sem("b_x2l")
        b_gate = sem("b_gate")
        b_top = sem("b_top")
        s_onerow = sem("s_onerow")
        c_gap = sem("c_gap")
        c_exp = sem("c_exp")
        c_dve = sem("c_dve")
        c_wd = sem("c_wd")
        s_wstat = sem("s_wstat")
        s_wtop = sem("s_wtop")
        w_t = sem("w_t")
        w_tc = sem("w_tc")
        b2_done = sem("b2_done")
        b2_used = sem("b2_used")
        z_done = sem("z_done")
        z_act = sem("z_act")
        g_hi = sem("g_hi")
        g_lo = sem("g_lo")
        y_prod = sem("y_prod")
        y_used = sem("y_used")
        d_dve = sem("d_dve")
        o_done = sem("o_done")
        o_out = [sem("o_out_a"), sem("o_out_b")]

        block = ctx.enter_context(nc.Block())

        def alone(eng, semaphore, value):
            eng.wait_ge(semaphore, value)
            eng.sem_inc(s_alone, 1)

        names = ["g0", "beta0", "wsum", "absb", "yb", "pyb", "sx", "isx", "pra", "sa", "isa", "bound", "pb",
                 "t", "it", "wscale", "rs", "g1", "beta1", "nbeta1", "absum", "ipyb", "ipra", "ipb", "isx2", "tmp",
                 "p1", "s1", "isz", "p2", "s2", "gb", "pg", "sg", "isy"]
        cols = {n: col[:, k:k + 1] for k, n in enumerate(names)}

        SMALL = [(ident, "ident"), (at32, "at"), (a32, "a"), (w0t, "w0t"), (bn0, "bn0"), (bn1, "bn1"), (w1, "w1")]
        LATE = [(causal, "causal"), (iota8, "iota8"), (w2, "w2"), (wq, "wq"), (wk, "wk"), (wv, "wv"), (wot, "wot"),
                (wg, "wg"), (eb1, "eb1"), (ew2, "ew2"), (eb2, "eb2")]

        @block.sync
        def _(sp):
            for t, name in SMALL:
                sp.dma_start(t[:, :], dram[name]).then_inc(s_par, 16)
            sp.dma_start(bn1row[:, :, :], dram["bn1t"].partition_broadcast(P)).then_inc(s_par, 16)
            sp.dma_start(bn2row[:, :, :], dram["bn2t"].partition_broadcast(P)).then_inc(s_par, 16)
            per = PADDED * CIN // XLOADS
            for n in range(XLOADS):
                sp.dma_start(xs[0:V, n * per:(n + 1) * per], dram["x"][:, n * per:(n + 1) * per]).then_inc(x_in[n], 16)
            for t, name in LATE:
                sp.dma_start(t[:, :], dram[name]).then_inc(s_late, 16)
            for k in range(2):
                sp.dma_start(ew1[k * D:k * D + D, :], dram["ew1"]).then_inc(s_late, 16)

            sp.wait_ge(s_asplit, 3)
            for b in range(BLOCKS):
                for row, rows, node, frame in SPANS[b]:
                    c0 = ABASE[b] + frame * V
                    for dst, src in ((ablkhi, ahi), (ablklo, alo)):
                        sp.dma_start(dst[row:row + rows, c0:c0 + V], src[node:node + rows, :]).then_inc(s_ablk, 16)

            def load_y(half):
                for k, part in enumerate((yhi, yhi, ylo, ylo)):
                    sp.dma_start(yt[CIN * k:CIN * k + CIN, half * HALF * V:(half + 1) * HALF * V],
                                 part[half * CIN * HALF:(half + 1) * CIN * HALF, :]).then_inc(yt_in[half], 16)

            sp.wait_ge(y_split, 1)
            load_y(0)
            load_y(1)
            with sp.Fori(0, ITERS - 1) as i:
                sp.wait_ge(y_split, i + 2)
                sp.wait_ge(l0_done, i * GROUPS + GROUPS // 2)
                load_y(0)
                sp.wait_ge(l0_done, i * GROUPS + GROUPS)
                load_y(1)

            with sp.Fori(0, QUADS) as j:
                for h in range(2):
                    sp.wait_ge(o_done, 2 * j + h + 1)
                    src = ofin[:, h * 2 * D:(h + 1) * 2 * D].rearrange("p (t d) -> p t d", t=2)
                    sp.dma_start(out[bass.ds(j * QUAD + 2 * h, 2), :, :].rearrange("t p d -> p t d"), src)\
                      .then_inc(o_out[h], 16)
            sp.wait_ge(o_out[0], 16 + 16 * QUADS)
            sp.wait_ge(o_out[1], 16 + 16 * QUADS)

        @block.gpsimd
        def _(pool):
            pool.wait_ge(s_stat, 1)
            pool.partition_all_reduce(top[:, :], stat[:, :], P, bass.bass_isa.ReduceOp.max).then_inc(s_top, 1)
            pool.tensor_copy(xcur[:, :], xs[0:V, 0:XCOLS]).then_inc(xcur_in, 1)
            with pool.Fori(0, ITERS - 1) as i:
                pool.wait_ge(y_mm, i + 1)
                pool.tensor_copy(xcur[:, :], xs[0:V, bass.ds(i * XCOLS + XCOLS, XCOLS)]).then_inc(xcur_in, 1)
            pool.wait_ge(s_wstat, 1)
            pool.partition_all_reduce(wtop[:, :], wstat[:, :], P, bass.bass_isa.ReduceOp.max).then_inc(s_wtop, 1)

        @block.scalar
        def _(act):
            def y_high(i):
                act.wait_ge(y_mm, i + 1)
                act.activation(yhi[:, :], bank[6][0:XCOLS, 0:V], ACT.Copy, scale=cols["sx"][0:XCOLS, :])\
                   .then_inc(y_hi_done, 1)

            def h0_high(G, s):
                act.wait_ge(l0_done, G + 1)
                act.activation(h0hi[:, s % 2, :], bank[s % 2][0:BLOCK, 0:BLOCKS * C], ACT.Relu).then_inc(hi_done, 1)

            def p_copy(G, s):
                act.wait_ge(a_done, G + 1)
                act.activation(pt[:, s % 2, :], bank[2 + s % 2][:, 0:GROUP], ACT.Copy).then_inc(p_copied, 1)

            act.wait_ge(s_var, 1)
            act.activation(root[:, :], vareps[:, :], ACT.Sqrt).then_inc(s_root, 1)
            act.wait_ge(s_set, 1)
            y_high(0)
            h0_high(0, 0)
            h0_high(1, 1)
            p_copy(0, 0)
            h0_high(2, 2)

            def body(i, last=False):
                for s in range(GROUPS):
                    G = i * GROUPS + s
                    if not (last and s + 1 >= GROUPS):
                        act.wait_ge(w1_done, G + 1)
                        p_copy(G + 1, s + 1)
                    if not (last and s + 3 >= GROUPS):
                        h0_high(G + 3, s + 3)
                    if s == 0 and not last:
                        act.wait_ge(yt_in[0], 64 * (i + 1))
                        act.wait_ge(yt_in[1], 64 * (i + 1))
                        y_high(i + 1)

            with act.Fori(0, ITERS - 1) as i:
                body(i)
            body(ITERS - 1, last=True)

            act.wait_ge(q_free, 2 + ITERS * GROUPS)
            with act.Fori(0, QUADS) as j:
                act.wait_ge(b_h, j + 1)
                act.activation(hb, hbar[:, bass.ds(j * QTOK, QTOK)], ACT.Copy).then_inc(hb_in, 1)
                act.wait_ge(b_var, 2 * j + 1)
                act.activation(rstd, ve, ACT.Sqrt).then_inc(b_root, 1)
                act.wait_ge(b_xt, j + 1)
                act.activation(xnt, bank[1][0:D, :], ACT.Copy).then_inc(b_xtc, 1)
                act.wait_ge(b_s, j + 1)
                act.activation(st, bank[2][0:D, :], ACT.Copy).then_inc(b_sc, 1)
                act.wait_ge(b_var, 2 * j + 2)
                act.activation(rstd, ve, ACT.Sqrt).then_inc(b_root, 1)
                act.wait_ge(b_x2t, j + 1)
                act.wait_ge(b_gate, j + 1)
                act.wait_ge(s_onerow, 1)
                act.activation(xn2q[0:D, :], bank[6][0:D, :], ACT.Copy).then_inc(b_x2c, 1)
                act.activation(xn2t[:, bass.ds(j * QTOK, QTOK)], bank[6][:, :], ACT.Copy, scale=XTOP)\
                   .then_inc(b_x2h, 1)

            act.wait_ge(c_gap, 1)
            act.activation(egap, gap, ACT.Exp).then_inc(c_exp, 1)

            for k in range(TILES // E):
                act.wait_ge(w_t, k + 1)
                if k >= 2:
                    act.wait_ge(b2_done, k - 1)
                act.activation(wdt[:, (k % 2) * TILE:(k % 2 + 1) * TILE], bank[k % 2][0:E * E, 0:TILE], ACT.Copy)\
                   .then_inc(w_tc, 1)

            buf = lambda e: slice(e % SPARE * QTOK, (e % SPARE + 1) * QTOK)

            def gelu_of(n, e):
                act.wait_ge(z_done, n + 1)
                act.wait_ge(g_lo, n + 1)
                act.activation(gelu[:, buf(e)], bank[e % SPARE][:, :], ACT.Gelu, scale=cols["isz"],
                               bias=eb1[:, e:e + 1]).then_inc(z_act, 1)

            def gelu_high(n, e):
                act.wait_ge(z_act, SPARE + n + 1)
                act.wait_ge(y_prod, n + 1)
                act.activation(ghi[:, buf(e)], gelu[:, buf(e)], ACT.Copy, scale=cols["sg"]).then_inc(g_hi, 1)

            with act.Fori(0, QUADS) as j:
                for e in range(CHUNKS):
                    gelu_of(j * CHUNKS + e, e)
                    if e > 0:
                        gelu_high(j * CHUNKS + e - 1, e - 1)
                gelu_high(j * CHUNKS + CHUNKS - 1, CHUNKS - 1)

        @block.vector
        def _(v):
            links = [0]

            def link(ins):
                links[0] += 1
                ins.then_inc(s_chain, 1)
                v.wait_ge(s_chain, links[0])

            c = cols
            v.memset(ones[:, :], 1.0).then_inc(s_ones, 1)
            v.memset(ablkhi[:, :], 0.0).then_inc(s_asplit, 1)
            v.memset(ablklo[:, :], 0.0).then_inc(s_asplit, 1)
            v.sem_inc(q_done, 2)
            v.sem_inc(q_free, 2)
            v.sem_inc(y_used, 2)
            v.sem_inc(z_act, SPARE)
            v.sem_inc(g_lo, SPARE)
            v.sem_inc(y_prod, SPARE)
            v.sem_inc(b_x2l, 1)
            v.sem_inc(w1_done, 1)
            v.sem_inc(b_h, 1)
            v.sem_inc(b_gate, 1)
            v.sem_inc(o_out[0], 16)
            v.sem_inc(o_out[1], 16)
            link(v.memset(yt[:, :], 1.0))
            link(v.memset(stat[:, :], 0.0))
            v.wait_ge(s_par, 16 * (len(SMALL) + 2))
            link(v.tensor_copy(ident16[:, :], ident[:, :]))
            link(v.tensor_reduce(stat[0:V, 1:2], a32[:, :], X, ALU.add, apply_absolute_value=True))

            for k, var in ((0, bn0[:, 4:5]), (1, bn1[:, 4:5])):
                link(v.tensor_scalar(vareps[:, k:k + 1], var, EPS, None, ALU.add))
            link(v.tensor_scalar(vareps[:, 2:2 + C], bn1row[:, 4, :], EPS, None, ALU.add))
            v.tensor_scalar(vareps[:, 2 + C:], bn2row[:, 4, :], EPS, None, ALU.add).then_inc(s_var, 1)
            v.wait_ge(s_root, 1)
            link(v.reciprocal(root[:, :], root[:, :]))
            link(v.scalar_tensor_tensor(newton[:, :], root[:, :], -0.5, root[:, :], ALU.mult, ALU.mult))
            link(v.tensor_tensor(newton[:, :], newton[:, :], vareps[:, :], ALU.mult))
            link(v.scalar_tensor_tensor(root[:, :], newton[:, :], 1.5, root[:, :], ALU.add, ALU.mult))

            def batchnorm(b, inverse, gain, beta):
                link(v.tensor_tensor(gain, inverse, b[1], ALU.mult))
                if beta is not None:
                    link(v.tensor_tensor(beta, b[0], b[3], ALU.subtract))
                    link(v.tensor_tensor(beta, beta, gain, ALU.mult))
                    link(v.tensor_tensor(beta, beta, b[2], ALU.add))

            batchnorm([bn0[:, k:k + 1] for k in range(5)], root[:, 0:1], c["g0"], c["beta0"])
            batchnorm([bn1[:, k:k + 1] for k in range(5)], root[:, 1:2], c["g1"], c["beta1"])
            batchnorm([bn1row[:, k, :] for k in range(5)], root[:, 2:2 + C], g1row[:, :], None)
            batchnorm([bn2row[:, k, :] for k in range(5)], root[:, 2 + C:], g2row[:, :], bias2[:, :])
            link(v.tensor_scalar(c["nbeta1"], c["beta1"], -1.0, None, ALU.mult))
            link(v.tensor_scalar(w4[:, 0:CIN], w0t[:, :], c["g0"], None, ALU.mult))
            link(v.tensor_reduce(c["wsum"], w4[:, 0:CIN], X, ALU.add, apply_absolute_value=True))
            link(v.tensor_reduce(c["absb"], c["beta0"], X, ALU.add, apply_absolute_value=True))
            per = PADDED * CIN // XLOADS
            for n in range(XLOADS):
                v.wait_ge(x_in[n], 16)
                link(v.tensor_reduce(xmax[0:V, n:n + 1], xs[0:V, n * per:(n + 1) * per], X, ALU.max,
                                     apply_absolute_value=True))
            v.tensor_reduce(stat[0:V, 0:1], xmax[0:V, :], X, ALU.max).then_inc(s_stat, 1)
            v.wait_ge(s_top, 1)

            def power_of_two(dst, src):
                link(v.tensor_scalar(dst, src, TINY, None, ALU.max))
                link(v.tensor_single_scalar(dst.bitcast(U32), dst.bitcast(U32), 0x7F800000, ALU.bitwise_and))

            power_of_two(c["pra"], top[:, 1:2])
            link(v.reciprocal(c["ipra"], c["pra"]))
            link(v.tensor_scalar(c["sa"], c["ipra"], ATOP, None, ALU.mult))
            link(v.tensor_scalar(ascaled[:, :], at32[:, :], c["sa"][0:V, :], None, ALU.mult))
            link(v.tensor_copy(ahi[:, :], ascaled[:, :]))
            v.tensor_tensor(alo[:, :], ascaled[:, :], ahi[:, :], ALU.subtract).then_inc(s_asplit, 1)
            link(v.tensor_tensor(c["yb"], top[:, 0:1], top[:, 1:2], ALU.mult))
            link(v.tensor_scalar(c["yb"], c["yb"], SLACK, None, ALU.mult))
            power_of_two(c["pyb"], c["yb"])
            link(v.reciprocal(c["ipyb"], c["pyb"]))
            link(v.tensor_scalar(c["sx"], c["ipyb"], YTOP, None, ALU.mult))
            link(v.tensor_scalar(c["isx"], c["pyb"], 1.0 / YTOP, None, ALU.mult))
            link(v.scalar_tensor_tensor(c["bound"], c["wsum"], c["yb"], c["absb"], ALU.mult, ALU.add))
            link(v.tensor_scalar(c["bound"], c["bound"], SLACK, None, ALU.mult))
            power_of_two(c["pb"], c["bound"])
            link(v.reciprocal(c["ipb"], c["pb"]))
            link(v.tensor_scalar(c["t"], c["ipb"], HTOP, None, ALU.mult))
            link(v.tensor_tensor(c["wscale"], c["t"], c["isx"], ALU.mult))
            link(v.tensor_scalar(w4[:, 0:CIN], w4[:, 0:CIN], c["wscale"], None, ALU.mult))
            link(v.tensor_tensor(w4[:, 3:4], c["beta0"], c["t"], ALU.mult))
            link(v.tensor_copy(w4hi[:, :], w4[:, :]))
            link(v.tensor_tensor(w4lo[:, :], w4[:, :], w4hi[:, :], ALU.subtract))
            for k, part in enumerate((w4hi, w4lo, w4hi, w4lo)):
                link(v.tensor_copy(w0cols[:, CIN * k:CIN * k + CIN], part[:, 0:CIN]))
            link(v.tensor_copy(w0cols[:, 12:13], w4hi[:, 3:4]))
            v.tensor_copy(w0cols[:, 13:14], w4lo[:, 3:4]).then_inc(s_w0c, 1)
            link(v.tensor_scalar(c["it"], c["pb"], 1.0 / HTOP, None, ALU.mult))
            link(v.tensor_scalar(c["isa"], c["pra"], 1.0 / ATOP, None, ALU.mult))
            link(v.tensor_tensor(c["rs"], c["it"], c["isa"], ALU.mult))
            link(v.scalar_tensor_tensor(w1s[:, :], w1[:, :], c["rs"], g1row[:, :], ALU.mult, ALU.mult))
            v.wait_ge(s_w0t, 1)
            v.tensor_copy(w0x[:, :], bank[7][0:YROWS, 0:C // 2].bitcast(F16)).then_inc(s_w0x, 1)
            v.wait_ge(s_abar, 1)
            for k in range(FRAMES):
                link(v.tensor_scalar(abar[:, k, :], bank[5][:, 0:V], 1.0 / V, None, ALU.mult))
            v.sem_inc(s_set, 1)

            def y_low(i):
                v.wait_ge(y_hi_done, i + 1)
                v.scalar_tensor_tensor(ylo[:, :], bank[6][0:XCOLS, 0:V], c["sx"][0:XCOLS, :], yhi[:, :],
                                       ALU.mult, ALU.subtract).then_inc(y_split, 1)

            def h0_low(G, s):
                v.wait_ge(hi_done, G + 1)
                v.scalar_tensor_tensor(h0lo[:, s % 2, :], bank[s % 2][0:BLOCK, 0:BLOCKS * C], 0.0, h0hi[:, s % 2, :],
                                       ALU.max, ALU.subtract).then_inc(split_done, 1)

            y_low(0)
            h0_low(0, 0)
            h0_low(1, 1)
            h0_low(2, 2)

            def body(i, last=False):
                for s in range(GROUPS):
                    G = i * GROUPS + s
                    v.wait_ge(w1_done, G + 2)
                    v.wait_ge(q_free, G + 1)
                    v.scalar_tensor_tensor(q[:, s % 2, :], bank[4 + s % 2][:, 0:GROUP], c["nbeta1"],
                                           abar[:, :, :].rearrange("p f u -> p (f u)"), ALU.max, ALU.mult)\
                     .then_inc(q_done, 1)
                    if not (last and s + 3 >= GROUPS):
                        h0_low(G + 3, s + 3)
                    v.wait_ge(q_done, G + 3)
                    v.tensor_reduce(hbar[:, bass.ds(i * STEP + s * FRAMES, FRAMES)],
                                    q[:, s % 2, :].rearrange("p (f u) -> p f u", u=V), X, ALU.add).then_inc(q_free, 1)
                    if s == 0 and not last:
                        y_low(i + 1)

            with v.Fori(0, ITERS - 1) as i:
                body(i)
            body(ITERS - 1, last=True)

            v.wait_ge(s_late, 16 * (len(LATE) + 2))
            link(v.tensor_tensor(w2s[:, :], w2[:, :], g2row[:, :], ALU.mult))
            link(v.tensor_reduce(c["absum"], abar[:, 0, :], X, ALU.add))
            link(v.tensor_tensor(c["tmp"], c["absum"], c["beta1"], ALU.mult))
            v.tensor_scalar(corr[:, :], ones[:, :], c["tmp"], None, ALU.mult).then_inc(s_corr, 1)
            v.wait_ge(s_mmset, 1)
            link(v.tensor_tensor(bias2[:, :], bias2[:, :], bank[7][:, 0:D], ALU.add))
            link(v.tensor_copy(mqk[:, :], bank[7][0:D, D:2 * D]))
            link(v.tensor_copy(nvo[:, :], bank[7][0:D, 2 * D:3 * D]))
            v.sem_inc(s_ready, 1)
            v.memset(xn2q[D:D + 1, :], 1.0).then_inc(s_onerow, 1)
            v.wait_ge(q_free, 2 + ITERS * GROUPS)
            v.wait_ge(s_onerow, 1)

            link(v.tensor_reduce(wstat[:, 0:1], ew1[:, :], X, ALU.max, apply_absolute_value=True))
            link(v.tensor_reduce(wstat[:, 1:2], ew2[:, :], X, ALU.max, apply_absolute_value=True))
            v.tensor_reduce(wstat[:, 2:3], eb1[:, :], X, ALU.max, apply_absolute_value=True).then_inc(s_wstat, 1)
            v.wait_ge(s_wtop, 1)
            for w, hi, lo, k, p, scale in ((ew1, w1hi, w1lo, 0, "p1", "s1"), (ew2, w2hi, w2lo, 1, "p2", "s2")):
                power_of_two(c[p], wtop[:, k:k + 1])
                link(v.reciprocal(c[scale], c[p]))
                link(v.tensor_scalar(c[scale], c[scale], HTOP, None, ALU.mult))
                link(v.tensor_scalar(w[:, :], w[:, :], c[scale], None, ALU.mult))
                link(v.tensor_copy(hi, w[:, :]))
                link(v.tensor_tensor(lo, w[:, :], hi, ALU.subtract))
            link(v.tensor_scalar(c["isz"], c["p1"], 1.0 / (HTOP * XTOP), None, ALU.mult))
            link(v.scalar_tensor_tensor(c["gb"], wtop[:, 0:1], float(D) * 1.01, wtop[:, 2:3], ALU.mult, ALU.add))
            power_of_two(c["pg"], c["gb"])
            link(v.reciprocal(c["sg"], c["pg"]))
            link(v.tensor_scalar(c["sg"], c["sg"], HTOP, None, ALU.mult))
            link(v.tensor_scalar(c["isy"], c["pg"], 1.0 / HTOP, None, ALU.mult))
            link(v.scalar_tensor_tensor(c["isy"], c["isy"], 1.0 / HTOP, c["p2"], ALU.mult, ALU.mult))

            def norm(j, which_norm, base, k, dst, src, copies=1):
                for t in range(QUAD):
                    v.bn_stats(bn[:, 6 * t:6 * t + 6], src[:, t * D:(t + 1) * D]).then_inc(b_dve, 1)
                alone(v, b_dve, base + k + QUAD)
                for t in range(QUAD):
                    v.bn_aggr(mv[:, 2 * t:2 * t + 2], bn[:, 6 * t:6 * t + 6]).then_inc(b_dve, 1)
                v.wait_ge(b_dve, base + k + 2 * QUAD)
                v.tensor_scalar(ve, mv.rearrange("p (t s) -> p t s", s=2)[:, :, 1], EPS, None, ALU.add).then_inc(b_var, 1)
                v.wait_ge(b_root, 2 * j + which_norm + 1)
                v.reciprocal(rstd, rstd).then_inc(b_dve, 1)
                k += 2 * QUAD + 1
                v.wait_ge(b_dve, base + k)
                v.scalar_tensor_tensor(nt, rstd, -0.5, rstd, ALU.mult, ALU.mult).then_inc(b_dve, 1)
                k += 1
                v.wait_ge(b_dve, base + k)
                v.tensor_tensor(nt, nt, ve, ALU.mult).then_inc(b_dve, 1)
                k += 1
                v.wait_ge(b_dve, base + k)
                v.scalar_tensor_tensor(rstd, nt, 1.5, rstd, ALU.add, ALU.mult).then_inc(b_dve, 1)
                k += 1
                v.wait_ge(b_dve, base + k)
                for t in range(QUAD):
                    to, by = dst[:, t * copies * D:(t + 1) * copies * D], src[:, t * D:(t + 1) * D]
                    if copies > 1:
                        to = to.rearrange("p (k d) -> p k d", k=copies)
                        by = by.unsqueeze(1).broadcast_to([P, copies, D])
                    last = v.tensor_scalar(to, by, mv[:, 2 * t:2 * t + 1], rstd[:, t:t + 1], ALU.subtract, ALU.mult)
                    if t < QUAD - 1:
                        last.then_inc(b_dve, 1)
                return last, k + QUAD - 1

            STEPS = 1 + 2 * (3 * QUAD + 3) + 1 + 1 + 2 * QUAD
            with v.Fori(0, QUADS) as j:
                base = j * STEPS
                v.wait_ge(b_h, j + 2)
                v.tensor_tensor(hs.rearrange("p (t d) -> p t d", t=QUAD),
                                bank[0][:, 0:QUAD * D].rearrange("p (t d) -> p t d", t=QUAD),
                                bias2[:, :].unsqueeze(1).broadcast_to([P, QUAD, D]), ALU.add).then_inc(b_dve, 1)
                v.wait_ge(b_dve, base + 1)
                last, k = norm(j, 0, base, 1, xn, hs)
                last.then_inc(b_xn, 1)
                v.wait_ge(b_vo, j + 1)
                v.tensor_copy(vo, bank[3][:, 0:QUAD * D]).then_inc(b_voc, 1)
                v.wait_ge(b_lg, j + 1)
                v.scalar_tensor_tensor(attn.rearrange("p (t l) -> p t l", t=QUAD),
                                       bank[4][:, :].rearrange("p (t l) -> p t l", t=QUAD), 0.0,
                                       causal[:, :].unsqueeze(1).broadcast_to([P, QUAD, TILE]), ALU.max, ALU.mult)\
                 .then_inc(b_at, 1)
                v.wait_ge(b_cx, j + 1)
                v.tensor_tensor(h2, hs, bank[5][:, 0:QUAD * D], ALU.add).then_inc(b_dve, 1)
                k += 1
                v.wait_ge(b_dve, base + k)
                v.tensor_copy(h2all[:, bass.ds(j * QUAD * D, QUAD * D)], h2).then_inc(b_h2, 1)
                last, k = norm(j, 1, base, k, xn2, h2, copies=2)
                last.then_inc(b_xn2, 1)
                v.wait_ge(b_x2h, j + 1)
                low = xn2t[D:2 * D, bass.ds(j * QTOK, QTOK)]
                v.scalar_tensor_tensor(low, bank[6][D:2 * D, :], XTOP, low, ALU.mult, ALU.subtract).then_inc(b_x2l, 1)
                v.wait_ge(b_gate, j + 2)
                v.tensor_copy(gl, bank[7][:, 0:QUAD * E]).then_inc(b_dve, 1)
                k += 1
                alone(v, b_dve, base + k)
                for t in range(QUAD):
                    v.max(mx[:, 8 * t:8 * t + 8], gl[:, E * t:E * t + E]).then_inc(b_dve, 1)
                    k += 1
                alone(v, b_dve, base + k)
                for t in range(QUAD):
                    v.max_index(mi[:, 8 * t:8 * t + 8], mx[:, 8 * t:8 * t + 8], gl[:, E * t:E * t + E]).then_inc(b_dve, 1)
                    k += 1
                v.wait_ge(b_dve, base + k)
                first = lambda a: a.rearrange("p (t k) -> p t k", k=8)[:, :, 0:2]
                v.tensor_copy(best[:, bass.ds(j * QUAD * 2, QUAD * 2)].rearrange("p (t k) -> p t k", k=2), first(mx))\
                 .then_inc(b_top, 1)
                v.tensor_copy(which[:, bass.ds(j * QUAD * 2, QUAD * 2)].rearrange("p (t k) -> p t k", k=2), first(mi))\
                 .then_inc(b_top, 1)
                v.wait_ge(b_top, 2 * j + 2)
                v.wait_ge(b_h2, j + 1)
                assert k == STEPS

            n = [0]

            def step(ins):
                n[0] += 1
                ins.then_inc(c_dve, 1)
                v.wait_ge(c_dve, n[0])

            pair = best.rearrange("p (t k) -> p t k", k=2)
            v.tensor_tensor(gap, pair[:, :, 1], pair[:, :, 0], ALU.subtract).then_inc(c_gap, 1)
            v.wait_ge(c_exp, 1)
            step(v.tensor_scalar(den, egap, 1.0, None, ALU.add))
            step(v.reciprocal(prob[:, 0:TILES], den))
            step(v.tensor_tensor(prob[:, TILES:2 * TILES], prob[:, 0:TILES], egap, ALU.mult))
            wd3 = wd.rearrange("p (t e) -> p t e", e=E)
            hit3 = hit.rearrange("p (t e) -> p t e", e=E)
            expert = iota8[:, :].unsqueeze(1).broadcast_to([P, TILES, E])
            chosen = which.rearrange("p (t k) -> p t k", k=2)
            for k, dst in enumerate((wd3, hit3)):
                step(v.tensor_tensor(dst, expert, chosen[:, :, k:k + 1].broadcast_to([P, TILES, E]), ALU.is_equal))
                step(v.tensor_tensor(dst, dst, prob[:, k * TILES:(k + 1) * TILES].unsqueeze(2)
                                     .broadcast_to([P, TILES, E]), ALU.mult))
            step(v.tensor_tensor(wd, wd, hit, ALU.add))
            v.sem_inc(c_wd, 1)

            for k in range(TILES // E):
                v.wait_ge(b2_done, k + 1)
                part = h2all[:, k * E * D:(k + 1) * E * D]
                v.tensor_tensor(part, part, bank[2 + k % 2][:, :], ALU.add).then_inc(b2_used, 1)
            step(v.tensor_scalar(wds, wd, c["isy"], None, ALU.mult))
            v.wait_ge(b2_used, TILES // E)

            buf = lambda e: slice(e % SPARE * QTOK, (e % SPARE + 1) * QTOK)

            def gelu_low(j, e):
                n = j * CHUNKS + e
                v.wait_ge(g_hi, n + 1)
                v.wait_ge(y_prod, n + 1)
                v.scalar_tensor_tensor(glo[:, buf(e)], gelu[:, buf(e)], c["sg"], ghi[:, buf(e)],
                                       ALU.mult, ALU.subtract).then_inc(g_lo, 1)

            WEIGHS = 12

            def weigh(j, half, pair, k):
                if pair == 0:
                    v.wait_ge(y_prod, SPARE + j * CHUNKS + (half + 1) * CHUNKS // 2)
                for t in range(2):
                    tile_no = 2 * pair + t
                    dst = ycomb[:, tile_no * E * D + half * E // 2 * D:tile_no * E * D + (half + 1) * E // 2 * D]
                    src = bank[4 + 2 * half + pair][:, t * E // 2 * D:(t + 1) * E // 2 * D]
                    w = wds[:, bass.ds((j * QUAD + tile_no) * E + half * E // 2, E // 2)]
                    v.tensor_tensor(dst.rearrange("p (e d) -> p e d", e=E // 2),
                                    src.rearrange("p (e d) -> p e d", e=E // 2),
                                    w.unsqueeze(2).broadcast_to([P, E // 2, D]), ALU.mult).then_inc(d_dve, 1)
                v.wait_ge(d_dve, j * WEIGHS + 2 * k + 2)
                if pair == 1:
                    v.sem_inc(y_used, 1)

            def add_up(j, pair):
                for t in range(2):
                    tile_no = 2 * pair + t
                    yc = ycomb[:, tile_no * E * D:(tile_no + 1) * E * D]
                    v.tensor_reduce(osum[:, tile_no * D:(tile_no + 1) * D], yc.rearrange("p (e d) -> p d e", e=E),
                                    X, ALU.add).then_inc(d_dve, 1)
                v.wait_ge(d_dve, j * WEIGHS + 8 + 2 * pair + 2)
                v.wait_ge(o_out[pair], 16 * j + 16)
                v.tensor_tensor(ofin[:, pair * 2 * D:(pair + 1) * 2 * D], osum[:, pair * 2 * D:(pair + 1) * 2 * D],
                                h2all[:, bass.ds((j * QUAD + 2 * pair) * D, 2 * D)], ALU.add).then_inc(o_done, 1)

            def body(j, behind):
                for e in range(CHUNKS):
                    gelu_low(j, e)
                    if behind and e in (2, 3):
                        weigh(j - 1, 1, e - 2, e)
                    if behind and e in (5, 7):
                        add_up(j - 1, (e - 5) // 2)
                    if e in (10, 11):
                        weigh(j, 0, e - 10, e - 10)

            body(0, behind=False)
            with v.Fori(1, QUADS) as j:
                body(j, behind=True)
            weigh(QUADS - 1, 1, 0, 2)
            weigh(QUADS - 1, 1, 1, 3)
            add_up(QUADS - 1, 0)
            add_up(QUADS - 1, 1)

        @block.tensor
        def _(pe):
            def y_product(i):
                pe.wait_ge(xcur_in, i + 1)
                pe.matmul(bank[6][0:XCOLS, 0:V], xcur[:, :], at32[:, :], start=True, stop=True).then_inc(y_mm, 1)

            def l0(s):
                g = s % GROUPS
                for b in range(BLOCKS):
                    n = (g * BLOCKS + b) * BLOCK
                    mm = pe.matmul(bank[s % 2][0:BLOCK, b * C:(b + 1) * C], yt[:, n:n + BLOCK], w0x[:, :],
                                   start=True, stop=True, skip_group_check=True)
                mm.then_inc(l0_done, 1)

            def a_product(s):
                first = True
                for b in range(BLOCKS):
                    width = len(SPANS[b]) * V
                    c0 = FIRST_FRAME[b] * V
                    for h, a in ((h0hi, ablkhi), (h0hi, ablklo), (h0lo, ablkhi)):
                        mm = pe.matmul(bank[2 + s % 2][:, c0:c0 + width], h[:, s % 2, b * C:(b + 1) * C],
                                       a[0:BLOCK, ABASE[b]:ABASE[b] + width], start=first,
                                       stop=(b == BLOCKS - 1 and h is h0lo), skip_group_check=True)
                        first = False
                mm.then_inc(a_done, 1)

            def w1_product(s):
                pe.matmul(bank[4 + s % 2][:, 0:GROUP], w1s[:, :], pt[:, s % 2, :], start=True, stop=True)\
                  .then_inc(w1_done, 1)

            pe.wait_ge(s_ones, 1)
            pe.wait_ge(s_par, 16 * (len(SMALL) + 2))
            pe.matmul(bank[5][:, 0:V], ones[0:V, :], a32[:, :], start=True, stop=True).then_inc(s_abar, 1)
            pe.wait_ge(s_w0c, 1)
            pe.transpose(bank[7][0:YROWS, 0:C // 2].bitcast(F16), w0cols[:, :], ident16[:, :]).then_inc(s_w0t, 1)
            pe.wait_ge(s_w0x, 1)
            y_product(0)
            pe.wait_ge(s_ablk, 16 * 2 * sum(len(x) for x in SPANS))
            pe.wait_ge(s_set, 1)
            pe.wait_ge(yt_in[0], 64)
            l0(0)
            l0(1)
            pe.wait_ge(split_done, 1)
            a_product(0)
            l0(2)

            def body(i, last=False):
                for s in range(GROUPS):
                    G = i * GROUPS + s
                    if not (last and s + 1 >= GROUPS):
                        pe.wait_ge(split_done, G + 2)
                        a_product(s + 1)
                    if s == 1:
                        pe.wait_ge(yt_in[1], 64 * (i + 1))
                    if s == 5 and not last:
                        pe.wait_ge(yt_in[0], 64 * (i + 2))
                    if not (last and s + 3 >= GROUPS):
                        l0(s + 3)
                    if s == 0 and not last:
                        y_product(i + 1)
                    pe.wait_ge(p_copied, G + 1)
                    pe.wait_ge(q_done, G + 1)
                    w1_product(s)

            with pe.Fori(0, ITERS - 1) as i:
                body(i)
            body(ITERS - 1, last=True)

            pe.wait_ge(s_corr, 1)
            pe.matmul(bank[7][:, 0:D], corr[:, :], w2s[:, :], start=True, stop=True, skip_group_check=True)
            pe.matmul(bank[7][0:D, D:2 * D], wq[:, :], wk[:, :], start=True, stop=True, skip_group_check=True)
            pe.matmul(bank[7][0:D, 2 * D:3 * D], wv[:, :], wot[:, :], start=True, stop=True, skip_group_check=True)\
              .then_inc(s_mmset, 1)
            pe.wait_ge(s_ready, 1)

            tok = lambda t: slice(t * TILE, (t + 1) * TILE)
            ch = lambda t: slice(t * D, (t + 1) * D)
            with pe.Fori(0, QUADS) as j:
                pe.wait_ge(hb_in, j + 1)
                for t in range(QUAD):
                    mm = pe.matmul(bank[0][:, ch(t)], hb[:, tok(t)], w2s[:, :], start=True, stop=True)
                mm.then_inc(b_h, 1)
                alone(pe, b_xn, j + 1)
                for t in range(QUAD):
                    mm = pe.transpose(bank[1][0:D, tok(t)], xn[:, ch(t)], ident[:, :])
                mm.then_inc(b_xt, 1)
                alone(pe, b_xtc, j + 1)
                pe.matmul(bank[2][0:D, :], mqk[:, :], xnt, start=True, stop=True).then_inc(b_s, 1)
                for t in range(QUAD):
                    mm = pe.matmul(bank[3][:, ch(t)], xnt[:, tok(t)], nvo[:, :], start=True, stop=True)
                mm.then_inc(b_vo, 1)
                pe.wait_ge(b_sc, j + 1)
                for t in range(QUAD):
                    mm = pe.matmul(bank[4][:, tok(t)], xnt[:, tok(t)], st[:, tok(t)], start=True, stop=True)
                mm.then_inc(b_lg, 1)
                pe.wait_ge(b_voc, j + 1)
                pe.wait_ge(b_at, j + 1)
                for t in range(QUAD):
                    mm = pe.matmul(bank[5][:, ch(t)], attn[:, tok(t)], vo[:, ch(t)], start=True, stop=True)
                mm.then_inc(b_cx, 1)
                alone(pe, b_xn2, j + 1)
                pe.wait_ge(b_x2l, j + 1)
                for t in range(QUAD):
                    mm = pe.transpose(bank[6][:, tok(t)], xn2[:, 2 * t * D:2 * (t + 1) * D], ident[:, :])
                mm.then_inc(b_x2t, 1)
                pe.wait_ge(b_x2c, j + 1)
                for t in range(QUAD):
                    mm = pe.matmul(bank[7][:, t * E:(t + 1) * E], xn2q[:, tok(t)], wg[:, :], start=True, stop=True)
                mm.then_inc(b_gate, 1)

            pe.wait_ge(c_wd, 1)

            def transpose_weights(k):
                if k >= 2:
                    pe.wait_ge(w_tc, k - 1)
                pe.transpose(bank[k % 2][0:E * E, 0:TILE], wd[:, k * E * E:(k + 1) * E * E], ident[:, :])\
                  .then_inc(w_t, 1)

            transpose_weights(0)
            for k in range(TILES // E):
                if k + 1 < TILES // E:
                    transpose_weights(k + 1)
                pe.wait_ge(w_tc, k + 1)
                if k >= 2:
                    pe.wait_ge(b2_used, k - 1)
                pe.matmul(bank[2 + k % 2][:, :], wdt[:, (k % 2) * TILE:(k % 2 + 1) * TILE], eb2[:, :],
                          start=True, stop=True).then_inc(b2_done, 1)

            pe.wait_ge(b2_used, TILES // E)
            pe.wait_ge(b_x2l, 1 + QUADS)
            pe.wait_ge(b_top, 2 * QUADS)

            def z_product(j, e):
                pe.wait_ge(z_act, j * CHUNKS + e + 1)
                for w in (w1hi, w1lo):
                    mm = pe.matmul(bank[e % SPARE][:, :], w[:, e * P:(e + 1) * P], xn2t[:, bass.ds(j * QTOK, QTOK)],
                                   start=(w is w1hi), stop=(w is w1lo))
                mm.then_inc(z_done, 1)

            def y_product(j, e):
                pe.wait_ge(g_lo, SPARE + j * CHUNKS + e + 1)
                half, expert = e // E, e // 2 % (E // 2)
                if e % E == 0:
                    pe.wait_ge(y_used, 2 * j + half + 1)
                for t in range(QUAD):
                    at = (t % 2) * E // 2 * D + expert * D
                    b0 = e % SPARE * QTOK + t * TILE
                    for g, w in ((ghi, w2hi), (ghi, w2lo), (glo, w2hi)):
                        mm = pe.matmul(bank[4 + 2 * half + t // 2][:, at:at + D], g[:, b0:b0 + TILE],
                                       w[:, e * D:(e + 1) * D],
                                       start=(e % E == 0 and t % 2 == 0 and g is ghi and w is w2hi),
                                       stop=(e % E == E - 1 and t % 2 == 1 and g is glo), skip_group_check=True)
                mm.then_inc(y_prod, 1)

            AHEAD = 3
            for e in range(AHEAD):
                z_product(0, e)

            def body(j, last=False):
                for e in range(CHUNKS):
                    if e + AHEAD < CHUNKS:
                        z_product(j, e + AHEAD)
                    elif not last:
                        z_product(j + 1, e + AHEAD - CHUNKS)
                    y_product(j, e)

            with pe.Fori(0, QUADS - 1) as j:
                body(j)
            body(QUADS - 1, last=True)


def kernel(**inputs):
    import numpy as _np
    import concourse.bacc as _bacc
    from concourse.bass_utils import run_bass_kernel_spmd as _run

    g = {k: _np.ascontiguousarray(v) for k, v in inputs.items()}
    x = _np.zeros((PADDED, V, CIN), _np.float32)
    x[:TOKENS] = g["x"].reshape(TOKENS, V, CIN)
    bn = [_np.stack([g[f"L0_tok_{n}{i}"] for n in ("b", "g", "be", "m", "v")]) for i in range(3)]
    eb2 = _np.zeros((E, E, E, D), _np.float32)
    for k in range(E):
        eb2[k, :, k] = g["L0_ffn_b2"]
    token = _np.arange(TILE)
    allowed = (token[:, None] <= token[None, :]) & (token[:, None] // T == token[None, :] // T)
    arrays = {
        "x": x.reshape(2 * ITERS, HALF, V, CIN).transpose(2, 0, 3, 1).reshape(V, PADDED * CIN),
        "a": g["L0_tok_A"], "at": g["L0_tok_A"].T,
        "w0t": g["L0_tok_W0"].T, "w1": g["L0_tok_W1"], "w2": g["L0_tok_W2"],
        "bn0": bn[0].T, "bn1": bn[1].T, "bn1t": bn[1], "bn2t": bn[2],
        "wq": g["L0_attn_Wq"], "wk": g["L0_attn_Wk"], "wv": g["L0_attn_Wv"], "wot": g["L0_attn_Wo"].T,
        "wg": _np.concatenate([g["L0_ffn_Wg"], g["L0_ffn_bg"][None]]),
        "ew1": g["L0_ffn_W1"].transpose(1, 0, 2).reshape(D, E * H),
        "eb1": g["L0_ffn_b1"].reshape(CHUNKS, P).T,
        "ew2": g["L0_ffn_W2"].reshape(CHUNKS, P, D).transpose(1, 0, 2).reshape(P, CHUNKS * D),
        "eb2": eb2.reshape(E * E, E * D),
        "ident": _np.eye(P, dtype=_np.float32),
        "causal": (allowed / _np.maximum(token % T, 1)[None, :]).astype(_np.float32),
        "iota8": _np.tile(_np.arange(E, dtype=_np.float32), (P, 1)),
    }
    arrays = {f"in_{k}": _np.ascontiguousarray(v) for k, v in arrays.items()}
    nc = _bacc.Bacc("TRN2", target_bir_lowering=False, num_devices=1)
    dram = {k[3:]: nc.dram_tensor(k, v.shape, F32, kind="ExternalInput").ap() for k, v in arrays.items()}
    out = nc.dram_tensor("out_0", (TILES, TILE, D), F32, kind="ExternalOutput").ap()
    build(nc, dram, out)
    r = _run(nc, [arrays], core_ids=[0])
    return r.results[0]["out_0"].reshape(B, T, D)
```

```python
from contextlib import ExitStack

import numpy as np

import concourse.bass as bass
from concourse import mybir

F32 = mybir.dt.float32
F16 = mybir.dt.float16
U32 = mybir.dt.uint32
ALU = mybir.AluOpType
ACT = mybir.ActivationFunctionType
X = mybir.AxisListType.X

P = 128
EPS = 1e-5
B, T, V, CIN = 128, 64, 75, 3
C = 128
D = 64
E, H = 8, 256
TOKENS = B * T

FRAMES = 5
BLOCK = 125
BLOCKS = FRAMES * V // BLOCK
GROUP = FRAMES * V
GROUPS = 8
HALF = GROUPS // 2 * FRAMES
STEP = 2 * HALF
ITERS = -(-TOKENS // STEP)
PADDED = ITERS * STEP
XCOLS = 2 * CIN * HALF
XLOADS = 10
YROWS = 4 * CIN + 2
SPANS = [[(0, 75, 0, 0), (75, 50, 0, 1)],
         [(0, 25, 50, 0), (25, 75, 0, 1), (100, 25, 0, 2)],
         [(0, 50, 25, 0), (50, 75, 0, 1)]]
FIRST_FRAME = [0, 1, 3]
ABASE = [0, 2 * V, 5 * V]
ACOLS = 7 * V
YTOP, HTOP, ATOP = 2.0 ** 8, 2.0 ** 14, 2.0 ** 14
PSCALE = 2.0 ** -15
AWAY = [0, 3]
NEAR = [s for s in range(GROUPS) if s not in AWAY]
SUMS = {1: [(-1, [6, 7])], 2: [(-1, [3])], 4: [(0, [1, 2])], 5: [(0, [0])], 7: [(0, [4, 5])]}
PBUF = 4
HBUF = 4
TINY = 2.0 ** -60
SLACK = 1.001

TILE = 128
QUAD = 4
QTOK = QUAD * TILE
QUADS = TOKENS // QTOK
TILES = TOKENS // TILE
ROUNDS = QUADS // 2
RTILES = 2 * QUAD
CHUNKS = 2 * E
SPARE = 4
DVE_HIGH = [0, 4, 7, 9, 13]
ACT_HIGH = [e for e in range(CHUNKS) if e not in DVE_HIGH]
XTOP = 2.0 ** 10


def build(nc, dram, out):
    ctx = ExitStack()
    with ctx:
        def sb(name, shape, dt=F32):
            return ctx.enter_context(nc.sbuf_tensor(name, shape, dt))

        def sem(name):
            return ctx.enter_context(nc.semaphore(name))

        bank = [ctx.enter_context(nc.psum_tensor(f"bank{n}", [P, 512], F32)) for n in range(8)]

        xs = sb("xs", [P, PADDED * CIN])
        hbar = sb("hbar", [P, PADDED])
        ident = sb("ident", [P, P])
        ident16 = sb("ident16", [P, P], F16)
        causal = sb("causal", [P, P])
        iota8 = sb("iota8", [P, E])
        at32 = sb("at32", [V, V])
        a32 = sb("a32", [V, V])
        w0t = sb("w0t", [P, CIN])
        bn0 = sb("bn0", [P, 5])
        bn1 = sb("bn1", [P, 5])
        bn1row = sb("bn1row", [P, 5, C])
        bn2row = sb("bn2row", [P, 5, D])
        w1 = sb("w1", [P, C])
        w2 = sb("w2", [P, D])
        wq = sb("wq", [D, D])
        wk = sb("wk", [D, D])
        wv = sb("wv", [D, D])
        wot = sb("wot", [D, D])
        wg = sb("wg", [D + 1, E])
        ew1 = sb("ew1", [P, E * H])
        eb1 = sb("eb1", [P, CHUNKS])
        ew2 = sb("ew2", [P, CHUNKS * D])
        eb2 = sb("eb2", [E * E, E * D])
        stat = sb("stat", [P, 5])
        top = sb("top", [P, 5])
        wstat = sb("wstat", [P, 3])
        wtop = sb("wtop", [P, 3])
        xmax = sb("xmax", [P, XLOADS])
        col = sb("col", [P, 48])
        w4 = sb("w4", [P, 4])
        w4hi = sb("w4hi", [P, 4], F16)
        w4lo = sb("w4lo", [P, 4], F16)
        w0cols = sb("w0cols", [P, YROWS], F16)
        w0x = sb("w0x", [YROWS, C], F16)
        ascaled = sb("ascaled", [V, V])
        ahi = sb("ahi", [V, V], F16)
        alo = sb("alo", [V, V], F16)
        ablkhi = sb("ablkhi", [P, ACOLS], F16)
        ablklo = sb("ablklo", [P, ACOLS], F16)
        vareps = sb("vareps", [P, 2 + C + D])
        root = sb("root", [P, 2 + C + D])
        newton = sb("newton", [P, 2 + C + D])
        g1row = sb("g1row", [P, C])
        w1s = sb("w1s", [P, C])
        w1shi = sb("w1shi", [P, C], F16)
        w1slo = sb("w1slo", [P, C], F16)
        g2row = sb("g2row", [P, D])
        w2s = sb("w2s", [P, D])
        ones = sb("ones", [P, P])
        abar = sb("abar", [P, FRAMES, V])
        corr = sb("corr", [P, P])
        bias2 = sb("bias2", [P, D])
        mqk = sb("mqk", [D, D])
        nvo = sb("nvo", [D, D])
        xcur = sb("xcur", [V, XCOLS])
        yhi = sb("yhi", [XCOLS, V], F16)
        ylo = sb("ylo", [XCOLS, V], F16)
        yt = sb("yt", [YROWS, STEP * V], F16)
        h0hi = sb("h0hi", [BLOCK, HBUF, BLOCKS * C], F16)
        h0lo = sb("h0lo", [BLOCK, HBUF, BLOCKS * C], F16)
        pt = sb("pt", [P, PBUF, GROUP])
        pthi = sb("pthi", [P, PBUF, GROUP], F16)
        ptlo = sb("ptlo", [P, PBUF, GROUP], F16)
        h1away = sb("h1away", [P, GROUP])
        qaway = sb("qaway", [P, len(AWAY), GROUP])
        q = sb("q", [P, len(NEAR), GROUP])

        at = 0

        def again(cols, rows=P):
            nonlocal at
            view = xs[0:rows, at:at + cols]
            at += cols
            return view

        h2all = again(TILES * D)
        xn2t = again(TOKENS // 2).bitcast(F16)
        attention_at = at
        hb = again(2 * QTOK)
        hs = again(RTILES * D)
        bn = again(RTILES * 6)
        mv = [again(RTILES * 2), again(RTILES * 2)]
        ve = again(RTILES)
        rstd = again(RTILES)
        nt = again(RTILES)
        xn = again(RTILES * D)
        xnt = again(2 * QTOK, D)
        st = again(2 * QTOK, D)
        vo = again(RTILES * D)
        attn = again(2 * QTOK)
        h2 = again(RTILES * D)
        xc2 = again(RTILES * D)
        xn2 = again(RTILES * 2 * D)
        xn2q = again(2 * QTOK, D + 1)
        gl = again(RTILES * E)
        mx = again(RTILES * 8)
        mi = again(RTILES * 8).bitcast(U32)
        best_at = at
        best = again(TILES * 2)
        which = again(TILES * 2)
        gap = again(TILES)
        egap = again(TILES)
        prob = again(2 * TILES)
        den = again(TILES)
        hit = again(TILES * E)
        wd = again(TILES * E)
        wds = again(TILES * E)
        w1hi = again(E * H // 2).bitcast(F16)
        w1lo = again(E * H // 2).bitcast(F16)
        w2hi = again(CHUNKS * D // 2).bitcast(F16)
        w2lo = again(CHUNKS * D // 2).bitcast(F16)
        wdt = again(2 * TILE, E * E)
        osum = again(QUAD * D)
        ofin = again(QUAD * D)
        assert at <= PADDED * CIN
        at = attention_at
        gelu = again(SPARE * QTOK)
        ghi = again(SPARE * QTOK // 2).bitcast(F16)
        glo = again(SPARE * QTOK // 2).bitcast(F16)
        ycomb = again(QUAD * E * D)
        assert at <= best_at

        s_par = sem("s_par")
        s_late = sem("s_late")
        x_in = [sem(f"x_in{n}") for n in range(XLOADS)]
        s_chain = sem("s_chain")
        s_stat = sem("s_stat")
        s_top = sem("s_top")
        s_asplit = sem("s_asplit")
        s_ablk = sem("s_ablk")
        s_w0c = sem("s_w0c")
        s_w0t = sem("s_w0t")
        s_w0x = sem("s_w0x")
        s_ones = sem("s_ones")
        s_abar = sem("s_abar")
        s_set = sem("s_set")
        s_var = sem("s_var")
        s_root = sem("s_root")
        s_corr = sem("s_corr")
        s_mmset = sem("s_mmset")
        s_ready = sem("s_ready")
        s_alone = sem("s_alone")
        xcur_in = sem("xcur_in")
        y_mm = sem("y_mm")
        y_hi_done = sem("y_hi_done")
        y_split = sem("y_split")
        yt_in = [sem("yt_in_a"), sem("yt_in_b")]
        l0_done = sem("l0_done")
        hi_done = sem("hi_done")
        split_done = sem("split_done")
        a_done = sem("a_done")
        p_copied = sem("p_copied")
        p_low = sem("p_low")
        w1_done = sem("w1_done")
        q_done = sem("q_done")
        q_free = sem("q_free")
        away_h1 = sem("away_h1")
        away_q = sem("away_q")
        away_free = sem("away_free")
        hbar_done = sem("hbar_done")
        hb_in = sem("hb_in")
        b_h = sem("b_h")
        b_dve = sem("b_dve")
        b_own = sem("b_own")
        b_var = sem("b_var")
        b_root = sem("b_root")
        b_xn = sem("b_xn")
        b_xt = sem("b_xt")
        b_xtc = sem("b_xtc")
        b_s = sem("b_s")
        b_vo = sem("b_vo")
        b_sc = sem("b_sc")
        b_voc = sem("b_voc")
        b_lg = sem("b_lg")
        b_at = sem("b_at")
        b_cx = sem("b_cx")
        b_h2 = sem("b_h2")
        b_h2c = sem("b_h2c")
        b_xn2 = sem("b_xn2")
        b_x2t = sem("b_x2t")
        b_x2c = sem("b_x2c")
        b_x2h = sem("b_x2h")
        b_x2l = sem("b_x2l")
        b_gate = sem("b_gate")
        b_gl = sem("b_gl")
        b_top = sem("b_top")
        s_onerow = sem("s_onerow")
        c_gap = sem("c_gap")
        c_exp = sem("c_exp")
        c_dve = sem("c_dve")
        c_wd = sem("c_wd")
        s_wstat = sem("s_wstat")
        s_wtop = sem("s_wtop")
        w_t = sem("w_t")
        w_tc = sem("w_tc")
        b2_done = sem("b2_done")
        b2_used = sem("b2_used")
        z_done = sem("z_done")
        z_act = sem("z_act")
        g_hi = sem("g_hi")
        g_dvehi = sem("g_dvehi")
        g_lo = sem("g_lo")
        y_prod = sem("y_prod")
        y_used = sem("y_used")
        d_dve = sem("d_dve")
        y_summed = sem("y_summed")
        d_pool = sem("d_pool")
        o_done = sem("o_done")
        o_out = [sem("o_out_a"), sem("o_out_b")]

        block = ctx.enter_context(nc.Block())

        def alone(eng, semaphore, value):
            eng.wait_ge(semaphore, value)
            eng.sem_inc(s_alone, 1)

        names = ["g0", "beta0", "wsum", "absb", "yb", "pyb", "sx", "isx", "pra", "sa", "isa", "bound", "pb",
                 "t", "it", "wscale", "rs", "g1", "beta1", "nbeta1", "absum", "ipyb", "ipra", "ipb", "tmp",
                 "bm", "pbm", "wb", "pw", "k1", "z1", "p1", "s1", "isz", "p2", "s2", "gb", "pg", "sg", "isy"]
        cols = {n: col[:, k:k + 1] for k, n in enumerate(names)}

        SMALL = [(ident, "ident"), (at32, "at"), (a32, "a"), (w0t, "w0t"), (bn0, "bn0"), (bn1, "bn1"), (w1, "w1")]
        LATE = [(causal, "causal"), (iota8, "iota8"), (w2, "w2"), (wq, "wq"), (wk, "wk"), (wv, "wv"), (wot, "wot"),
                (wg, "wg"), (eb1, "eb1"), (ew2, "ew2"), (eb2, "eb2")]

        @block.sync
        def _(sp):
            for t, name in SMALL:
                sp.dma_start(t[:, :], dram[name]).then_inc(s_par, 16)
            sp.dma_start(bn1row[:, :, :], dram["bn1t"].partition_broadcast(P)).then_inc(s_par, 16)
            sp.dma_start(bn2row[:, :, :], dram["bn2t"].partition_broadcast(P)).then_inc(s_par, 16)
            per = PADDED * CIN // XLOADS
            for n in range(XLOADS):
                sp.dma_start(xs[0:V, n * per:(n + 1) * per], dram["x"][:, n * per:(n + 1) * per]).then_inc(x_in[n], 16)
            for t, name in LATE:
                sp.dma_start(t[:, :], dram[name]).then_inc(s_late, 16)
            for k in range(2):
                sp.dma_start(ew1[k * D:k * D + D, :], dram["ew1"]).then_inc(s_late, 16)

            sp.wait_ge(s_asplit, 3)
            for b in range(BLOCKS):
                for row, rows, node, frame in SPANS[b]:
                    c0 = ABASE[b] + frame * V
                    for dst, src in ((ablkhi, ahi), (ablklo, alo)):
                        sp.dma_start(dst[row:row + rows, c0:c0 + V], src[node:node + rows, :]).then_inc(s_ablk, 16)

            def load_y(half):
                for k, part in enumerate((yhi, yhi, ylo, ylo)):
                    sp.dma_start(yt[CIN * k:CIN * k + CIN, half * HALF * V:(half + 1) * HALF * V],
                                 part[half * CIN * HALF:(half + 1) * CIN * HALF, :]).then_inc(yt_in[half], 16)

            def load_x(columns):
                sp.dma_start(xcur[:, :], xs[0:V, columns]).then_inc(xcur_in, 16)

            sp.wait_ge(s_stat, 1)
            load_x(slice(0, XCOLS))
            sp.wait_ge(y_mm, 1)
            load_x(slice(XCOLS, 2 * XCOLS))
            sp.wait_ge(y_split, 1)
            load_y(0)
            load_y(1)

            def iteration(i, more_x=True):
                if more_x:
                    sp.wait_ge(y_mm, i + 2)
                    load_x(bass.ds(i * XCOLS + 2 * XCOLS, XCOLS))
                sp.wait_ge(y_split, i + 2)
                sp.wait_ge(l0_done, i * GROUPS + GROUPS // 2)
                load_y(0)
                sp.wait_ge(l0_done, i * GROUPS + GROUPS)
                load_y(1)

            with sp.Fori(0, ITERS - 2) as i:
                iteration(i)
            iteration(ITERS - 2, more_x=False)

            with sp.Fori(0, QUADS) as j:
                for h in range(2):
                    sp.wait_ge(o_done, 2 * j + h + 1)
                    src = ofin[:, h * 2 * D:(h + 1) * 2 * D].rearrange("p (t d) -> p t d", t=2)
                    sp.dma_start(out[bass.ds(j * QUAD + 2 * h, 2), :, :].rearrange("t p d -> p t d"), src)\
                      .then_inc(o_out[h], 16)
            sp.wait_ge(o_out[0], 16 + 16 * QUADS)
            sp.wait_ge(o_out[1], 16 + 16 * QUADS)

        @block.gpsimd
        def _(pool):
            pool.wait_ge(s_stat, 1)
            pool.partition_all_reduce(top[:, :], stat[:, :], P, bass.bass_isa.ReduceOp.max).then_inc(s_top, 1)
            def p_low_part(G, s):
                pool.wait_ge(p_copied, 2 * G + 2)
                pool.tensor_tensor(ptlo[:, s % PBUF, :], pt[:, s % PBUF, :], pthi[:, s % PBUF, :], ALU.subtract)\
                    .then_inc(p_low, 1)

            p_low_part(0, 0)

            def weigh_away(i, s):
                k = AWAY.index(s)
                pool.wait_ge(away_h1, i * len(AWAY) + k + 1)
                if not (isinstance(i, int) and i == 0):
                    pool.wait_ge(away_free, (i - 1) * len(AWAY) + k + 1)
                pool.tensor_tensor(qaway[:, k, :], h1away[:, :], abar[:, :, :].rearrange("p f u -> p (f u)"),
                                   ALU.mult).then_inc(away_q, 1)

            def body(i, first=False, last=False):
                for s in range(GROUPS):
                    if not (last and s + 1 >= GROUPS):
                        p_low_part(i * GROUPS + s + 1, s + 1)
                    if (s - 2) % GROUPS in AWAY and not (first and s < 2):
                        weigh_away(i if s >= 2 else i - 1, (s - 2) % GROUPS)

            body(0, first=True)
            with pool.Fori(1, ITERS - 1) as i:
                body(i)
            body(ITERS - 1, last=True)

            pool.wait_ge(s_wstat, 1)
            pool.partition_all_reduce(wtop[:, :], wstat[:, :], P, bass.bass_isa.ReduceOp.max).then_inc(s_wtop, 1)

            pool.wait_ge(hbar_done, len(AWAY))

            def hb_copy(j):
                for k in range(2):
                    pool.wait_ge(b_h, 2 * j + k + 1)
                    pool.tensor_copy(hb[:, k * QTOK:(k + 1) * QTOK], hbar[:, bass.ds((2 * j + k) * QTOK, QTOK)])\
                        .then_inc(hb_in, 1)

            def h2_copy(j):
                for k in range(2):
                    pool.wait_ge(b_h2, 2 * j + k + 1)
                    pool.tensor_copy(h2all[:, bass.ds((2 * j + k) * QUAD * D, QUAD * D)],
                                     h2[:, k * QUAD * D:(k + 1) * QUAD * D]).then_inc(b_h2c, 1)

            hb_copy(0)
            with pool.Fori(0, ROUNDS - 1) as j:
                hb_copy(j + 1)
                h2_copy(j)
            h2_copy(ROUNDS - 1)

            pool.wait_ge(b2_used, TILES // E)
            with pool.Fori(0, QUADS) as j:
                for pair in range(2):
                    yc = ycomb[:, pair * 2 * E * D:(pair + 1) * 2 * E * D].rearrange("p (t e) -> p t e", t=2)
                    total = osum[:, pair * 2 * D:(pair + 1) * 2 * D]
                    pool.wait_ge(d_dve, 8 * j + 6 + 2 * pair)
                    left = E * D
                    for step in range(3):
                        left //= 2
                        dst = total.rearrange("p (t d) -> p t d", t=2) if step == 2 else yc[:, :, 0:left]
                        ins = pool.tensor_tensor(dst, yc[:, :, 0:left], yc[:, :, left:2 * left], ALU.add)
                        if step < 2:
                            ins.then_inc(d_pool, 1)
                            pool.wait_ge(d_pool, 4 * j + 2 * pair + step + 1)
                        else:
                            ins.then_inc(y_summed, 1)
                            pool.wait_ge(y_summed, 2 * j + pair + 3)
                    pool.wait_ge(o_out[pair], 16 * j + 16)
                    pool.tensor_tensor(ofin[:, pair * 2 * D:(pair + 1) * 2 * D], total,
                                       h2all[:, bass.ds((j * QUAD + 2 * pair) * D, 2 * D)], ALU.add).then_inc(o_done, 1)


        @block.scalar
        def _(act):
            def y_high(i):
                act.wait_ge(y_mm, i + 1)
                act.activation(yhi[:, :], bank[6][0:XCOLS, 0:V], ACT.Copy, scale=cols["sx"][0:XCOLS, :])\
                   .then_inc(y_hi_done, 1)

            def h0_high(G, s):
                act.wait_ge(l0_done, G + 1)
                act.activation(h0hi[:, s % HBUF, :], bank[s % 2][0:BLOCK, 0:BLOCKS * C], ACT.Relu).then_inc(hi_done, 1)

            def p_copy(G, s):
                act.wait_ge(a_done, G + 1)
                for dst in (pt, pthi):
                    act.activation(dst[:, s % PBUF, :], bank[2 + s % 2][:, 0:GROUP], ACT.Copy, scale=PSCALE)\
                       .then_inc(p_copied, 1)

            def h1_away(i, s):
                k = i * len(AWAY) + AWAY.index(s)
                act.wait_ge(w1_done, i * GROUPS + s + 1)
                if not (isinstance(k, int) and k == 0):
                    act.wait_ge(away_q, k)
                act.activation(h1away[:, :], bank[4 + s % 2][:, 0:GROUP], ACT.Relu, bias=cols["beta1"])\
                   .then_inc(away_h1, 1)

            act.wait_ge(s_var, 1)
            act.activation(root[:, :], vareps[:, :], ACT.Sqrt).then_inc(s_root, 1)
            act.wait_ge(s_set, 1)
            y_high(0)
            h0_high(0, 0)
            h0_high(1, 1)
            p_copy(0, 0)
            h0_high(2, 2)

            def body(i, first=False, last=False):
                for s in range(GROUPS):
                    G = i * GROUPS + s
                    if not (last and s + 3 >= GROUPS):
                        h0_high(G + 3, s + 3)
                    if (s - 2) % GROUPS in AWAY and not (first and s < 2):
                        h1_away(i if s >= 2 else i - 1, (s - 2) % GROUPS)
                    if s == 0 and not last:
                        act.wait_ge(yt_in[0], 64 * (i + 1))
                        act.wait_ge(yt_in[1], 64 * (i + 1))
                        y_high(i + 1)
                    if not (last and s + 1 >= GROUPS):
                        if not (first and s + 1 < PBUF):
                            act.wait_ge(w1_done, G + 2 - PBUF)
                        p_copy(G + 1, s + 1)

            body(0, first=True)
            with act.Fori(1, ITERS - 1) as i:
                body(i)
            body(ITERS - 1, last=True)

            act.wait_ge(hbar_done, len(AWAY))
            act.wait_ge(s_onerow, 1)
            part = lambda k: slice(k * QTOK, (k + 1) * QTOK)
            with act.Fori(0, ROUNDS) as j:
                act.wait_ge(b_var, 2 * j + 1)
                act.activation(rstd, ve, ACT.Sqrt).then_inc(b_root, 1)
                for k in range(2):
                    act.wait_ge(b_xt, 2 * j + k + 1)
                    act.activation(xnt[:, part(k)], bank[4 * k + 1][0:D, :], ACT.Copy).then_inc(b_xtc, 1)
                for k in range(2):
                    act.wait_ge(b_s, 2 * j + k + 1)
                    act.activation(st[:, part(k)], bank[4 * k + 2][0:D, :], ACT.Copy).then_inc(b_sc, 1)
                    act.wait_ge(b_vo, 2 * j + k + 1)
                    act.activation(vo[:, k * QUAD * D:(k + 1) * QUAD * D], bank[4 * k + 3][:, 0:QUAD * D], ACT.Copy)\
                       .then_inc(b_voc, 1)
                act.wait_ge(b_var, 2 * j + 2)
                act.activation(rstd, ve, ACT.Sqrt).then_inc(b_root, 1)
                for k in range(2):
                    act.wait_ge(b_x2t, 2 * j + k + 1)
                    act.activation(xn2q[0:D, part(k)], bank[4 * k + 2][0:D, :], ACT.Copy).then_inc(b_x2c, 1)
                    act.activation(xn2t[:, bass.ds((2 * j + k) * QTOK, QTOK)], bank[4 * k + 2][:, :], ACT.Copy,
                                   scale=XTOP).then_inc(b_x2h, 1)

            act.wait_ge(c_gap, 1)
            act.activation(egap, gap, ACT.Exp).then_inc(c_exp, 1)

            for k in range(TILES // E):
                act.wait_ge(w_t, k + 1)
                if k >= 2:
                    act.wait_ge(b2_done, k - 1)
                act.activation(wdt[:, (k % 2) * TILE:(k % 2 + 1) * TILE], bank[k % 2][0:E * E, 0:TILE], ACT.Copy)\
                   .then_inc(w_tc, 1)

            act.activation(egap, den, ACT.Gelu)
            buf = lambda e: slice(e % SPARE * QTOK, (e % SPARE + 1) * QTOK)

            def gelu_of(n, e):
                act.wait_ge(z_done, n + 1)
                act.wait_ge(g_lo, n + 1)
                act.activation(gelu[:, buf(e)], bank[e % SPARE][:, :], ACT.Gelu, scale=cols["isz"],
                               bias=eb1[:, e:e + 1]).then_inc(z_act, 1)

            def gelu_high(n, e):
                act.wait_ge(z_act, SPARE + n + 1)
                act.wait_ge(y_prod, n + 1)
                act.activation(ghi[:, buf(e)], gelu[:, buf(e)], ACT.Copy, scale=cols["sg"]).then_inc(g_hi, 1)

            with act.Fori(0, QUADS) as j:
                for e in range(CHUNKS):
                    gelu_of(j * CHUNKS + e, e)
                    if e > 0 and e - 1 not in DVE_HIGH:
                        gelu_high(j * CHUNKS + e - 1, e - 1)
                gelu_high(j * CHUNKS + CHUNKS - 1, CHUNKS - 1)

        @block.vector
        def _(v):
            links = [0]

            def link(ins):
                links[0] += 1
                ins.then_inc(s_chain, 1)
                v.wait_ge(s_chain, links[0])

            c = cols
            v.memset(ones[:, :], 1.0).then_inc(s_ones, 1)
            v.memset(ablkhi[:, :], 0.0).then_inc(s_asplit, 1)
            v.memset(ablklo[:, :], 0.0).then_inc(s_asplit, 1)
            v.sem_inc(y_used, 2)
            v.sem_inc(z_act, SPARE)
            v.sem_inc(g_lo, SPARE)
            v.sem_inc(y_prod, SPARE)
            v.sem_inc(b_h, 2)
            v.sem_inc(b_h2c, 2)
            v.sem_inc(y_summed, 2)
            v.sem_inc(b_gl, 2)
            v.sem_inc(o_out[0], 16)
            v.sem_inc(o_out[1], 16)
            link(v.memset(yt[:, :], 1.0))
            link(v.memset(stat[:, :], 0.0))
            v.wait_ge(s_par, 16 * (len(SMALL) + 2))
            link(v.tensor_copy(ident16[:, :], ident[:, :]))
            link(v.tensor_reduce(stat[0:V, 1:2], a32[:, :], X, ALU.add, apply_absolute_value=True))

            for k, var in ((0, bn0[:, 4:5]), (1, bn1[:, 4:5])):
                link(v.tensor_scalar(vareps[:, k:k + 1], var, EPS, None, ALU.add))
            link(v.tensor_scalar(vareps[:, 2:2 + C], bn1row[:, 4, :], EPS, None, ALU.add))
            v.tensor_scalar(vareps[:, 2 + C:], bn2row[:, 4, :], EPS, None, ALU.add).then_inc(s_var, 1)
            v.wait_ge(s_root, 1)
            link(v.reciprocal(root[:, :], root[:, :]))
            link(v.scalar_tensor_tensor(newton[:, :], root[:, :], -0.5, root[:, :], ALU.mult, ALU.mult))
            link(v.tensor_tensor(newton[:, :], newton[:, :], vareps[:, :], ALU.mult))
            link(v.scalar_tensor_tensor(root[:, :], newton[:, :], 1.5, root[:, :], ALU.add, ALU.mult))

            def batchnorm(b, inverse, gain, beta):
                link(v.tensor_tensor(gain, inverse, b[1], ALU.mult))
                if beta is not None:
                    link(v.tensor_tensor(beta, b[0], b[3], ALU.subtract))
                    link(v.tensor_tensor(beta, beta, gain, ALU.mult))
                    link(v.tensor_tensor(beta, beta, b[2], ALU.add))

            batchnorm([bn0[:, k:k + 1] for k in range(5)], root[:, 0:1], c["g0"], c["beta0"])
            batchnorm([bn1[:, k:k + 1] for k in range(5)], root[:, 1:2], c["g1"], c["beta1"])
            batchnorm([bn1row[:, k, :] for k in range(5)], root[:, 2:2 + C], g1row[:, :], None)
            batchnorm([bn2row[:, k, :] for k in range(5)], root[:, 2 + C:], g2row[:, :], bias2[:, :])
            link(v.tensor_tensor(w1s[:, :], w1[:, :], g1row[:, :], ALU.mult))
            link(v.tensor_reduce(stat[:, 2:3], w1s[:, :], X, ALU.max, apply_absolute_value=True))
            link(v.tensor_scalar(w4[:, 0:CIN], w0t[:, :], c["g0"], None, ALU.mult))
            link(v.tensor_reduce(c["wsum"], w4[:, 0:CIN], X, ALU.add, apply_absolute_value=True))
            link(v.tensor_reduce(c["absb"], c["beta0"], X, ALU.add, apply_absolute_value=True))
            link(v.tensor_copy(stat[:, 3:4], c["wsum"]))
            link(v.tensor_copy(stat[:, 4:5], c["absb"]))
            per = PADDED * CIN // XLOADS
            for n in range(XLOADS):
                v.wait_ge(x_in[n], 16)
                link(v.tensor_reduce(xmax[0:V, n:n + 1], xs[0:V, n * per:(n + 1) * per], X, ALU.max,
                                     apply_absolute_value=True))
            v.tensor_reduce(stat[0:V, 0:1], xmax[0:V, :], X, ALU.max).then_inc(s_stat, 1)
            v.wait_ge(s_top, 1)

            def power_of_two(dst, src):
                link(v.tensor_scalar(dst, src, TINY, None, ALU.max))
                link(v.tensor_single_scalar(dst.bitcast(U32), dst.bitcast(U32), 0x7F800000, ALU.bitwise_and))

            power_of_two(c["pra"], top[:, 1:2])
            link(v.reciprocal(c["ipra"], c["pra"]))
            link(v.tensor_scalar(c["sa"], c["ipra"], ATOP, None, ALU.mult))
            link(v.tensor_scalar(ascaled[:, :], at32[:, :], c["sa"][0:V, :], None, ALU.mult))
            link(v.tensor_copy(ahi[:, :], ascaled[:, :]))
            v.tensor_tensor(alo[:, :], ascaled[:, :], ahi[:, :], ALU.subtract).then_inc(s_asplit, 1)
            link(v.tensor_tensor(c["yb"], top[:, 0:1], top[:, 1:2], ALU.mult))
            link(v.tensor_scalar(c["yb"], c["yb"], SLACK, None, ALU.mult))
            power_of_two(c["pyb"], c["yb"])
            link(v.reciprocal(c["ipyb"], c["pyb"]))
            link(v.tensor_scalar(c["sx"], c["ipyb"], YTOP, None, ALU.mult))
            link(v.tensor_scalar(c["isx"], c["pyb"], 1.0 / YTOP, None, ALU.mult))
            link(v.scalar_tensor_tensor(c["bound"], c["wsum"], c["yb"], c["absb"], ALU.mult, ALU.add))
            link(v.tensor_scalar(c["bound"], c["bound"], SLACK, None, ALU.mult))
            power_of_two(c["pb"], c["bound"])
            link(v.reciprocal(c["ipb"], c["pb"]))
            link(v.tensor_scalar(c["t"], c["ipb"], HTOP, None, ALU.mult))
            link(v.tensor_tensor(c["wscale"], c["t"], c["isx"], ALU.mult))
            link(v.tensor_scalar(w4[:, 0:CIN], w4[:, 0:CIN], c["wscale"], None, ALU.mult))
            link(v.tensor_tensor(w4[:, 3:4], c["beta0"], c["t"], ALU.mult))
            link(v.tensor_copy(w4hi[:, :], w4[:, :]))
            link(v.tensor_tensor(w4lo[:, :], w4[:, :], w4hi[:, :], ALU.subtract))
            for k, part in enumerate((w4hi, w4lo, w4hi, w4lo)):
                link(v.tensor_copy(w0cols[:, CIN * k:CIN * k + CIN], part[:, 0:CIN]))
            link(v.tensor_copy(w0cols[:, 12:13], w4hi[:, 3:4]))
            v.tensor_copy(w0cols[:, 13:14], w4lo[:, 3:4]).then_inc(s_w0c, 1)
            link(v.tensor_scalar(c["it"], c["pb"], 1.0 / HTOP, None, ALU.mult))
            link(v.tensor_scalar(c["isa"], c["pra"], 1.0 / ATOP, None, ALU.mult))
            link(v.tensor_tensor(c["rs"], c["it"], c["isa"], ALU.mult))
            link(v.scalar_tensor_tensor(c["bm"], top[:, 3:4], c["yb"], top[:, 4:5], ALU.mult, ALU.add))
            link(v.tensor_scalar(c["bm"], c["bm"], SLACK, 1.0 / HTOP, ALU.mult, ALU.mult))
            power_of_two(c["pbm"], c["bm"])
            link(v.tensor_tensor(c["wb"], c["pbm"], c["isa"], ALU.mult))
            link(v.tensor_tensor(c["wb"], c["wb"], top[:, 2:3], ALU.mult))
            power_of_two(c["pw"], c["wb"])
            link(v.reciprocal(c["k1"], c["pw"]))
            link(v.tensor_scalar(c["k1"], c["k1"], HTOP, None, ALU.mult))
            link(v.tensor_scalar(w1s[:, :], w1s[:, :], c["rs"], c["k1"], ALU.mult, ALU.mult))
            link(v.tensor_copy(w1shi[:, :], w1s[:, :]))
            link(v.tensor_tensor(w1slo[:, :], w1s[:, :], w1shi[:, :], ALU.subtract))
            link(v.tensor_scalar(c["beta1"], c["beta1"], c["k1"], PSCALE, ALU.mult, ALU.mult))
            link(v.tensor_scalar(c["nbeta1"], c["beta1"], -1.0, None, ALU.mult))
            link(v.tensor_scalar(c["z1"], c["pw"], 1.0 / (HTOP * PSCALE), None, ALU.mult))
            v.wait_ge(s_w0t, 1)
            v.tensor_copy(w0x[:, :], bank[7][0:YROWS, 0:C // 2].bitcast(F16)).then_inc(s_w0x, 1)
            v.wait_ge(s_abar, 1)
            for k in range(FRAMES):
                link(v.tensor_scalar(abar[:, k, :], bank[5][:, 0:V], 1.0 / V, c["z1"], ALU.mult, ALU.mult))
            v.sem_inc(s_set, 1)

            def y_low(i):
                v.wait_ge(y_hi_done, i + 1)
                v.scalar_tensor_tensor(ylo[:, :], bank[6][0:XCOLS, 0:V], c["sx"][0:XCOLS, :], yhi[:, :],
                                       ALU.mult, ALU.subtract).then_inc(y_split, 1)

            def h0_low(G, s):
                v.wait_ge(hi_done, G + 1)
                v.scalar_tensor_tensor(h0lo[:, s % HBUF, :], bank[s % 2][0:BLOCK, 0:BLOCKS * C], 0.0, h0hi[:, s % HBUF, :],
                                       ALU.max, ALU.subtract).then_inc(split_done, 1)

            y_low(0)
            h0_low(0, 0)
            h0_low(1, 1)
            h0_low(2, 2)

            def weigh_h1(i, s):
                v.wait_ge(w1_done, i * GROUPS + s + 1)
                if not (isinstance(i, int) and i == 0):
                    v.wait_ge(q_free, (i - 1) * len(NEAR) + NEAR.index(s) + 1)
                v.scalar_tensor_tensor(q[:, NEAR.index(s), :], bank[4 + s % 2][:, 0:GROUP], c["nbeta1"],
                                       abar[:, :, :].rearrange("p f u -> p (f u)"), ALU.max, ALU.mult)\
                 .then_inc(q_done, 1)

            def sum_h1(i, groups):
                n = len(groups)
                frames = hbar[:, bass.ds(i * STEP + groups[0] * FRAMES, n * FRAMES)]
                for mine, src, made, done in ((AWAY, qaway, away_q, away_free), (NEAR, q, q_done, q_free)):
                    if groups[0] in mine:
                        k = mine.index(groups[0])
                        v.wait_ge(made, i * len(mine) + k + n)
                        v.tensor_reduce(frames, src[:, k:k + n, :].rearrange("p g (f u) -> p (g f) u", u=V), X, ALU.add)\
                         .then_inc(done, n)

            def body(i, first=False, last=False):
                for s in range(GROUPS):
                    before = (i - 1, GROUPS - 1) if s == 0 else (i, s - 1)
                    if not (last and s + 3 >= GROUPS):
                        h0_low(i * GROUPS + s + 3, s + 3)
                    for offset, groups in SUMS.get(s, []):
                        if not (first and offset < 0):
                            sum_h1(i + offset, groups)
                    if s == 0 and not last:
                        y_low(i + 1)
                    if before[1] in NEAR and not (first and s == 0):
                        weigh_h1(*before)

            body(0, first=True)
            with v.Fori(1, ITERS - 1) as i:
                body(i)
            body(ITERS - 1, last=True)
            weigh_h1(ITERS - 1, GROUPS - 1)
            for step in SUMS:
                for offset, groups in SUMS[step]:
                    if offset < 0:
                        sum_h1(ITERS - 1, groups)

            v.wait_ge(s_late, 16 * (len(LATE) + 2))
            link(v.tensor_tensor(w2s[:, :], w2[:, :], g2row[:, :], ALU.mult))
            link(v.tensor_reduce(c["absum"], abar[:, 0, :], X, ALU.add))
            link(v.tensor_tensor(c["tmp"], c["absum"], c["beta1"], ALU.mult))
            v.tensor_scalar(corr[:, :], ones[:, :], c["tmp"], None, ALU.mult).then_inc(s_corr, 1)
            v.wait_ge(q_free, ITERS * len(NEAR))
            v.wait_ge(away_free, ITERS * len(AWAY))
            for s in AWAY:
                away = hbar[:, :].rearrange("p (i f) -> p i f", f=STEP)[:, :, s * FRAMES:(s + 1) * FRAMES]
                v.tensor_scalar(away, away, c["tmp"], None, ALU.subtract).then_inc(hbar_done, 1)
            v.wait_ge(s_mmset, 1)
            link(v.tensor_tensor(bias2[:, :], bias2[:, :], bank[7][:, 0:D], ALU.add))
            link(v.tensor_copy(mqk[:, :], bank[7][0:D, D:2 * D]))
            link(v.tensor_copy(nvo[:, :], bank[7][0:D, 2 * D:3 * D]))
            v.sem_inc(s_ready, 1)
            v.memset(xn2q[D:D + 1, :], 1.0).then_inc(s_onerow, 1)
            v.wait_ge(s_onerow, 1)

            link(v.tensor_reduce(wstat[:, 0:1], ew1[:, :], X, ALU.max, apply_absolute_value=True))
            link(v.tensor_reduce(wstat[:, 1:2], ew2[:, :], X, ALU.max, apply_absolute_value=True))
            v.tensor_reduce(wstat[:, 2:3], eb1[:, :], X, ALU.max, apply_absolute_value=True).then_inc(s_wstat, 1)
            v.wait_ge(s_wtop, 1)
            for w, hi, lo, k, p, scale in ((ew1, w1hi, w1lo, 0, "p1", "s1"), (ew2, w2hi, w2lo, 1, "p2", "s2")):
                power_of_two(c[p], wtop[:, k:k + 1])
                link(v.reciprocal(c[scale], c[p]))
                link(v.tensor_scalar(c[scale], c[scale], HTOP, None, ALU.mult))
                link(v.tensor_scalar(w[:, :], w[:, :], c[scale], None, ALU.mult))
                link(v.tensor_copy(hi, w[:, :]))
                link(v.tensor_tensor(lo, w[:, :], hi, ALU.subtract))
            link(v.tensor_scalar(c["isz"], c["p1"], 1.0 / (HTOP * XTOP), None, ALU.mult))
            link(v.scalar_tensor_tensor(c["gb"], wtop[:, 0:1], float(D) * 1.01, wtop[:, 2:3], ALU.mult, ALU.add))
            power_of_two(c["pg"], c["gb"])
            link(v.reciprocal(c["sg"], c["pg"]))
            link(v.tensor_scalar(c["sg"], c["sg"], HTOP, None, ALU.mult))
            link(v.tensor_scalar(c["isy"], c["pg"], 1.0 / HTOP, None, ALU.mult))
            link(v.scalar_tensor_tensor(c["isy"], c["isy"], 1.0 / HTOP, c["p2"], ALU.mult, ALU.mult))

            order = [0]
            STEPS = 46

            def own(ins):
                order[0] += 1
                ins.then_inc(b_dve, 1)

            def settled(j, by_itself=False):
                if by_itself:
                    alone(v, b_dve, j * STEPS + order[0])
                else:
                    v.wait_ge(b_dve, j * STEPS + order[0])

            tiles = lambda k: slice(k * QUAD, (k + 1) * QUAD)
            chans = lambda k: slice(k * QUAD * D, (k + 1) * QUAD * D)
            by_tile = lambda a: a.rearrange("p (t d) -> p t d", d=D)

            def add_bias(j):
                for k in range(2):
                    v.wait_ge(b_h, 2 * j + k + 3)
                    own(v.tensor_tensor(by_tile(hs[:, chans(k)]), by_tile(bank[4 * k][:, 0:QUAD * D]),
                                        bias2[:, :].unsqueeze(1).broadcast_to([P, QUAD, D]), ALU.add))

            def moments(at, which_norm, src):
                settled(at)
                for t in range(RTILES):
                    own(v.bn_stats(bn[:, 6 * t:6 * t + 6], src[:, t * D:(t + 1) * D]))
                settled(at, by_itself=True)
                for t in range(RTILES):
                    own(v.bn_aggr(mv[which_norm][:, 2 * t:2 * t + 2], bn[:, 6 * t:6 * t + 6]))

            def center(at, j, which_norm, dst, src):
                settled(at)
                both = mv[which_norm].rearrange("p (t s) -> p t s", s=2)
                v.tensor_scalar(ve, both[:, :, 1], EPS, None, ALU.add).then_inc(b_var, 1)
                for k in range(2):
                    mean = both[:, tiles(k), 0:1].broadcast_to([P, QUAD, D])
                    own(v.tensor_tensor(by_tile(dst[:, chans(k)]), by_tile(src[:, chans(k)]), mean, ALU.subtract))
                v.wait_ge(b_root, 2 * j + which_norm + 1)
                own(v.reciprocal(rstd, rstd))
                settled(at)
                own(v.scalar_tensor_tensor(nt, rstd, -0.5, rstd, ALU.mult, ALU.mult))
                settled(at)
                own(v.tensor_tensor(nt, nt, ve, ALU.mult))
                settled(at)
                own(v.scalar_tensor_tensor(rstd, nt, 1.5, rstd, ALU.add, ALU.mult))
                settled(at)

            def choose(j):
                gates = 2 * RTILES
                for k in range(2):
                    v.wait_ge(b_gate, 2 * j + k + 1)
                    v.tensor_copy(gl[:, k * QUAD * E:(k + 1) * QUAD * E], bank[4 * k + 3][:, 0:QUAD * E])\
                     .then_inc(b_gl, 1)
                alone(v, b_gl, 2 * j + 4)
                for t in range(RTILES):
                    v.max(mx[:, 8 * t:8 * t + 8], gl[:, E * t:E * t + E]).then_inc(b_own, 1)
                alone(v, b_own, j * gates + RTILES)
                for t in range(RTILES):
                    v.max_index(mi[:, 8 * t:8 * t + 8], mx[:, 8 * t:8 * t + 8], gl[:, E * t:E * t + E]).then_inc(b_own, 1)
                v.wait_ge(b_own, j * gates + gates)
                first = lambda a: a.rearrange("p (t k) -> p t k", k=8)[:, :, 0:2]
                for dst, src in ((best, mx), (which, mi)):
                    v.tensor_copy(dst[:, bass.ds(j * RTILES * 2, RTILES * 2)].rearrange("p (t k) -> p t k", k=2),
                                  first(src)).then_inc(b_top, 1)
                v.wait_ge(b_top, 2 * j + 2)

            def body(j, first=False, last=False):
                order[0] = 2 + 2 * RTILES
                center(j, j, 0, xn, hs)
                for k in range(2):
                    by = rstd[:, tiles(k)].unsqueeze(2).broadcast_to([P, QUAD, D])
                    v.tensor_tensor(by_tile(xn[:, chans(k)]), by_tile(xn[:, chans(k)]), by, ALU.mult).then_inc(b_xn, 1)
                if not first:
                    choose(j - 1)
                for k in range(2):
                    v.wait_ge(b_lg, 2 * j + k + 1)
                    v.scalar_tensor_tensor(attn[:, k * QTOK:(k + 1) * QTOK].rearrange("p (t l) -> p t l", t=QUAD),
                                           bank[4 * k][:, :].rearrange("p (t l) -> p t l", t=QUAD), 0.0,
                                           causal[:, :].unsqueeze(1).broadcast_to([P, QUAD, TILE]), ALU.max, ALU.mult)\
                     .then_inc(b_at, 1)
                for k in range(2):
                    v.wait_ge(b_cx, 2 * j + k + 1)
                    v.wait_ge(b_h2c, 2 * j + k + 1)
                    v.tensor_tensor(h2[:, chans(k)], hs[:, chans(k)], bank[4 * k + 1][:, 0:QUAD * D], ALU.add)\
                     .then_inc(b_h2, 1)
                v.wait_ge(b_h2, 2 * j + 2)
                moments(j, 1, h2)
                center(j, j, 1, xc2, h2)
                for k in range(2):
                    by = rstd[:, tiles(k)].unsqueeze(2).unsqueeze(2).broadcast_to([P, QUAD, 2, D])
                    v.tensor_tensor(xn2[:, k * 2 * QUAD * D:(k + 1) * 2 * QUAD * D]
                                    .rearrange("p (t k d) -> p t k d", k=2, d=D),
                                    by_tile(xc2[:, chans(k)]).unsqueeze(2).broadcast_to([P, QUAD, 2, D]), by, ALU.mult)\
                     .then_inc(b_xn2, 1)
                assert order[0] == STEPS, order[0]
                order[0] = 0
                if not last:
                    add_bias(j + 1)
                    moments(j + 1, 0, hs)
                for k in range(2):
                    v.wait_ge(b_x2h, 2 * j + k + 1)
                    low = xn2t[D:2 * D, bass.ds((2 * j + k) * QTOK, QTOK)]
                    v.scalar_tensor_tensor(low, bank[4 * k + 2][D:2 * D, :], XTOP, low, ALU.mult, ALU.subtract)\
                     .then_inc(b_x2l, 1)

            add_bias(0)
            moments(0, 0, hs)
            body(0, first=True)
            with v.Fori(1, ROUNDS - 1) as j:
                body(j)
            body(ROUNDS - 1, last=True)
            choose(ROUNDS - 1)

            n = [0]

            def step(ins):
                n[0] += 1
                ins.then_inc(c_dve, 1)
                v.wait_ge(c_dve, n[0])

            pair = best.rearrange("p (t k) -> p t k", k=2)
            v.tensor_tensor(gap, pair[:, :, 1], pair[:, :, 0], ALU.subtract).then_inc(c_gap, 1)
            v.wait_ge(c_exp, 1)
            step(v.tensor_scalar(den, egap, 1.0, None, ALU.add))
            step(v.reciprocal(prob[:, 0:TILES], den))
            step(v.tensor_tensor(prob[:, TILES:2 * TILES], prob[:, 0:TILES], egap, ALU.mult))
            wd3 = wd.rearrange("p (t e) -> p t e", e=E)
            hit3 = hit.rearrange("p (t e) -> p t e", e=E)
            expert = iota8[:, :].unsqueeze(1).broadcast_to([P, TILES, E])
            chosen = which.rearrange("p (t k) -> p t k", k=2)
            for k, dst in enumerate((wd3, hit3)):
                step(v.tensor_tensor(dst, expert, chosen[:, :, k:k + 1].broadcast_to([P, TILES, E]), ALU.is_equal))
                step(v.tensor_tensor(dst, dst, prob[:, k * TILES:(k + 1) * TILES].unsqueeze(2)
                                     .broadcast_to([P, TILES, E]), ALU.mult))
            step(v.tensor_tensor(wd, wd, hit, ALU.add))
            v.sem_inc(c_wd, 1)

            v.wait_ge(b_h2c, 2 + QUADS)
            for k in range(TILES // E):
                v.wait_ge(b2_done, k + 1)
                part = h2all[:, k * E * D:(k + 1) * E * D]
                v.tensor_tensor(part, part, bank[2 + k % 2][:, :], ALU.add).then_inc(b2_used, 1)
            step(v.tensor_scalar(wds, wd, c["isy"], None, ALU.mult))
            v.wait_ge(b2_used, TILES // E)

            buf = lambda e: slice(e % SPARE * QTOK, (e % SPARE + 1) * QTOK)

            def gelu_low(j, e):
                n = j * CHUNKS + e
                v.wait_ge(y_prod, n + 1)
                if e in DVE_HIGH:
                    k = j * len(DVE_HIGH) + DVE_HIGH.index(e) + 1
                    v.wait_ge(z_act, SPARE + n + 1)
                    v.tensor_scalar(ghi[:, buf(e)], gelu[:, buf(e)], c["sg"], None, ALU.mult).then_inc(g_dvehi, 1)
                    v.wait_ge(g_dvehi, k)
                else:
                    v.wait_ge(g_hi, j * len(ACT_HIGH) + ACT_HIGH.index(e) + 1)
                v.scalar_tensor_tensor(glo[:, buf(e)], gelu[:, buf(e)], c["sg"], ghi[:, buf(e)],
                                       ALU.mult, ALU.subtract).then_inc(g_lo, 1)

            WEIGHS = 8

            def weigh(j, half, pair, k):
                if pair == 0:
                    v.wait_ge(y_prod, SPARE + j * CHUNKS + (half + 1) * CHUNKS // 2)
                v.wait_ge(y_summed, 2 * j + pair + 1)
                for t in range(2):
                    tile_no = 2 * pair + t
                    dst = ycomb[:, tile_no * E * D + half * E // 2 * D:tile_no * E * D + (half + 1) * E // 2 * D]
                    src = bank[4 + 2 * half + pair][:, t * E // 2 * D:(t + 1) * E // 2 * D]
                    w = wds[:, bass.ds((j * QUAD + tile_no) * E + half * E // 2, E // 2)]
                    v.tensor_tensor(dst.rearrange("p (e d) -> p e d", e=E // 2),
                                    src.rearrange("p (e d) -> p e d", e=E // 2),
                                    w.unsqueeze(2).broadcast_to([P, E // 2, D]), ALU.mult).then_inc(d_dve, 1)
                v.wait_ge(d_dve, j * WEIGHS + 2 * k + 2)
                if pair == 1:
                    v.sem_inc(y_used, 1)

            def body(j, behind):
                for e in range(CHUNKS):
                    gelu_low(j, e)
                    if behind and e in (2, 3):
                        weigh(j - 1, 1, e - 2, e)
                    if e in (10, 11):
                        weigh(j, 0, e - 10, e - 10)

            body(0, behind=False)
            with v.Fori(1, QUADS) as j:
                body(j, behind=True)
            weigh(QUADS - 1, 1, 0, 2)
            weigh(QUADS - 1, 1, 1, 3)

        @block.tensor
        def _(pe):
            def y_product(i):
                pe.wait_ge(xcur_in, 16 * i + 16)
                pe.matmul(bank[6][0:XCOLS, 0:V], xcur[:, :], at32[:, :], start=True, stop=True).then_inc(y_mm, 1)

            def l0(s):
                g = s % GROUPS
                for b in range(BLOCKS):
                    n = (g * BLOCKS + b) * BLOCK
                    mm = pe.matmul(bank[s % 2][0:BLOCK, b * C:(b + 1) * C], yt[:, n:n + BLOCK], w0x[:, :],
                                   start=True, stop=True, skip_group_check=True)
                mm.then_inc(l0_done, 1)

            def a_product(s):
                first = True
                for b in range(BLOCKS):
                    width = len(SPANS[b]) * V
                    c0 = FIRST_FRAME[b] * V
                    for h, a in ((h0hi, ablkhi), (h0hi, ablklo), (h0lo, ablkhi)):
                        mm = pe.matmul(bank[2 + s % 2][:, c0:c0 + width], h[:, s % HBUF, b * C:(b + 1) * C],
                                       a[0:BLOCK, ABASE[b]:ABASE[b] + width], start=first,
                                       stop=(b == BLOCKS - 1 and h is h0lo), skip_group_check=True)
                        first = False
                mm.then_inc(a_done, 1)

            def w1_product(i, s):
                pe.wait_ge(p_low, i * GROUPS + s + 1)
                j, r = (i - 1, s - 2 + GROUPS) if s < 2 else (i, s - 2)
                if not (isinstance(j, int) and j < 0):
                    if r in AWAY:
                        pe.wait_ge(away_h1, j * len(AWAY) + AWAY.index(r) + 1)
                    else:
                        pe.wait_ge(q_done, j * len(NEAR) + NEAR.index(r) + 1)
                for w, p in ((w1shi, pthi), (w1slo, pthi), (w1shi, ptlo)):
                    mm = pe.matmul(bank[4 + s % 2][:, 0:GROUP], w[:, :], p[:, s % PBUF, :],
                                   start=(w is w1shi and p is pthi), stop=(p is ptlo))
                mm.then_inc(w1_done, 1)

            pe.wait_ge(s_ones, 1)
            pe.wait_ge(s_par, 16 * (len(SMALL) + 2))
            pe.matmul(bank[5][:, 0:V], ones[0:V, :], a32[:, :], start=True, stop=True).then_inc(s_abar, 1)
            pe.wait_ge(s_w0c, 1)
            pe.transpose(bank[7][0:YROWS, 0:C // 2].bitcast(F16), w0cols[:, :], ident16[:, :]).then_inc(s_w0t, 1)
            pe.wait_ge(s_w0x, 1)
            y_product(0)
            pe.wait_ge(s_ablk, 16 * 2 * sum(len(x) for x in SPANS))
            pe.wait_ge(s_set, 1)
            pe.wait_ge(yt_in[0], 64)
            l0(0)
            l0(1)
            pe.wait_ge(split_done, 1)
            a_product(0)
            l0(2)

            def body(i, first=False, last=False):
                for s in range(GROUPS):
                    G = i * GROUPS + s
                    if s == 0 and not last:
                        y_product(i + 1)
                    if not (last and s + 1 >= GROUPS):
                        pe.wait_ge(split_done, G + 2)
                    if s == 1:
                        pe.wait_ge(yt_in[1], 64 * (i + 1))
                    if s == 5 and not last:
                        pe.wait_ge(yt_in[0], 64 * (i + 2))
                    if not (last and s + 3 >= GROUPS):
                        l0(s + 3)
                    if not (last and s + 1 >= GROUPS):
                        if not (first and s == 0):
                            pe.wait_ge(p_copied, 2 * G)
                        a_product(s + 1)
                    if not (first and s == 0):
                        w1_product(*((i - 1, GROUPS - 1) if s == 0 else (i, s - 1)))

            body(0, first=True)
            with pe.Fori(1, ITERS - 1) as i:
                body(i)
            body(ITERS - 1, last=True)
            w1_product(ITERS - 1, GROUPS - 1)

            pe.wait_ge(s_corr, 1)
            pe.matmul(bank[7][:, 0:D], corr[:, :], w2s[:, :], start=True, stop=True, skip_group_check=True)
            pe.matmul(bank[7][0:D, D:2 * D], wq[:, :], wk[:, :], start=True, stop=True, skip_group_check=True)
            pe.matmul(bank[7][0:D, 2 * D:3 * D], wv[:, :], wot[:, :], start=True, stop=True, skip_group_check=True)\
              .then_inc(s_mmset, 1)
            pe.wait_ge(s_ready, 1)

            tok = lambda t: slice(t * TILE, (t + 1) * TILE)
            ch = lambda t: slice(t * D, (t + 1) * D)

            def h_product(j):
                for k in range(2):
                    pe.wait_ge(hb_in, 2 * j + k + 1)
                    for t in range(QUAD):
                        mm = pe.matmul(bank[4 * k][:, ch(t)], hb[:, tok(k * QUAD + t)], w2s[:, :], start=True, stop=True)
                    mm.then_inc(b_h, 1)

            def body(j, last=False):
                for k in range(2):
                    alone(pe, b_xn, 2 * j + k + 1)
                    for t in range(QUAD):
                        mm = pe.transpose(bank[4 * k + 1][0:D, tok(t)], xn[:, ch(k * QUAD + t)], ident[:, :])
                    mm.then_inc(b_xt, 1)
                for k in range(2):
                    alone(pe, b_xtc, 2 * j + k + 1)
                    pe.matmul(bank[4 * k + 2][0:D, :], mqk[:, :], xnt[:, k * QTOK:(k + 1) * QTOK], start=True, stop=True)\
                      .then_inc(b_s, 1)
                for k in range(2):
                    pe.wait_ge(b_gl, 2 * j + k + 1)
                    for t in range(QUAD):
                        mm = pe.matmul(bank[4 * k + 3][:, ch(t)], xnt[:, tok(k * QUAD + t)], nvo[:, :], start=True, stop=True)
                    mm.then_inc(b_vo, 1)
                for k in range(2):
                    pe.wait_ge(b_sc, 2 * j + k + 1)
                    for t in range(QUAD):
                        mm = pe.matmul(bank[4 * k][:, tok(t)], xnt[:, tok(k * QUAD + t)], st[:, tok(k * QUAD + t)],
                                       start=True, stop=True)
                    mm.then_inc(b_lg, 1)
                for k in range(2):
                    pe.wait_ge(b_voc, 2 * j + k + 1)
                    pe.wait_ge(b_at, 2 * j + k + 1)
                    for t in range(QUAD):
                        mm = pe.matmul(bank[4 * k + 1][:, ch(t)], attn[:, tok(k * QUAD + t)], vo[:, ch(k * QUAD + t)],
                                       start=True, stop=True)
                    mm.then_inc(b_cx, 1)
                if not last:
                    h_product(j + 1)
                for k in range(2):
                    alone(pe, b_xn2, 2 * j + k + 1)
                    for t in range(QUAD):
                        u = k * QUAD + t
                        mm = pe.transpose(bank[4 * k + 2][:, tok(t)], xn2[:, 2 * u * D:2 * (u + 1) * D], ident[:, :])
                    mm.then_inc(b_x2t, 1)
                for k in range(2):
                    pe.wait_ge(b_x2c, 2 * j + k + 1)
                    for t in range(QUAD):
                        mm = pe.matmul(bank[4 * k + 3][:, t * E:(t + 1) * E], xn2q[:, tok(k * QUAD + t)], wg[:, :],
                                       start=True, stop=True)
                    mm.then_inc(b_gate, 1)

            h_product(0)
            with pe.Fori(0, ROUNDS - 1) as j:
                body(j)
            body(ROUNDS - 1, last=True)

            pe.wait_ge(c_wd, 1)

            def transpose_weights(k):
                if k >= 2:
                    pe.wait_ge(w_tc, k - 1)
                pe.transpose(bank[k % 2][0:E * E, 0:TILE], wd[:, k * E * E:(k + 1) * E * E], ident[:, :])\
                  .then_inc(w_t, 1)

            transpose_weights(0)
            for k in range(TILES // E):
                if k + 1 < TILES // E:
                    transpose_weights(k + 1)
                pe.wait_ge(w_tc, k + 1)
                if k >= 2:
                    pe.wait_ge(b2_used, k - 1)
                pe.matmul(bank[2 + k % 2][:, :], wdt[:, (k % 2) * TILE:(k % 2 + 1) * TILE], eb2[:, :],
                          start=True, stop=True).then_inc(b2_done, 1)

            pe.wait_ge(b2_used, TILES // E)
            pe.wait_ge(b_x2l, QUADS)
            pe.wait_ge(b_top, 2 * ROUNDS)

            def z_product(j, e):
                pe.wait_ge(z_act, j * CHUNKS + e + 1)
                for w in (w1hi, w1lo):
                    mm = pe.matmul(bank[e % SPARE][:, :], w[:, e * P:(e + 1) * P], xn2t[:, bass.ds(j * QTOK, QTOK)],
                                   start=(w is w1hi), stop=(w is w1lo))
                mm.then_inc(z_done, 1)

            def y_product(j, e):
                pe.wait_ge(g_lo, SPARE + j * CHUNKS + e + 1)
                half, expert = e // E, e // 2 % (E // 2)
                if e % E == 0:
                    pe.wait_ge(y_used, 2 * j + half + 1)
                for t in range(QUAD):
                    at = (t % 2) * E // 2 * D + expert * D
                    b0 = e % SPARE * QTOK + t * TILE
                    for g, w in ((ghi, w2hi), (ghi, w2lo), (glo, w2hi)):
                        mm = pe.matmul(bank[4 + 2 * half + t // 2][:, at:at + D], g[:, b0:b0 + TILE],
                                       w[:, e * D:(e + 1) * D],
                                       start=(e % E == 0 and t % 2 == 0 and g is ghi and w is w2hi),
                                       stop=(e % E == E - 1 and t % 2 == 1 and g is glo), skip_group_check=True)
                mm.then_inc(y_prod, 1)

            AHEAD = 3
            for e in range(AHEAD):
                z_product(0, e)

            def body(j, last=False):
                for e in range(CHUNKS):
                    if e + AHEAD < CHUNKS:
                        z_product(j, e + AHEAD)
                    elif not last:
                        z_product(j + 1, e + AHEAD - CHUNKS)
                    y_product(j, e)

            with pe.Fori(0, QUADS - 1) as j:
                body(j)
            body(QUADS - 1, last=True)


def kernel(**inputs):
    import numpy as _np
    import concourse.bacc as _bacc
    from concourse.bass_utils import run_bass_kernel_spmd as _run

    g = {k: _np.ascontiguousarray(v) for k, v in inputs.items()}
    x = _np.zeros((PADDED, V, CIN), _np.float32)
    x[:TOKENS] = g["x"].reshape(TOKENS, V, CIN)
    bn = [_np.stack([g[f"L0_tok_{n}{i}"] for n in ("b", "g", "be", "m", "v")]) for i in range(3)]
    eb2 = _np.zeros((E, E, E, D), _np.float32)
    for k in range(E):
        eb2[k, :, k] = g["L0_ffn_b2"]
    token = _np.arange(TILE)
    allowed = (token[:, None] <= token[None, :]) & (token[:, None] // T == token[None, :] // T)
    arrays = {
        "x": x.reshape(2 * ITERS, HALF, V, CIN).transpose(2, 0, 3, 1).reshape(V, PADDED * CIN),
        "a": g["L0_tok_A"], "at": g["L0_tok_A"].T,
        "w0t": g["L0_tok_W0"].T, "w1": g["L0_tok_W1"], "w2": g["L0_tok_W2"],
        "bn0": bn[0].T, "bn1": bn[1].T, "bn1t": bn[1], "bn2t": bn[2],
        "wq": g["L0_attn_Wq"], "wk": g["L0_attn_Wk"], "wv": g["L0_attn_Wv"], "wot": g["L0_attn_Wo"].T,
        "wg": _np.concatenate([g["L0_ffn_Wg"], g["L0_ffn_bg"][None]]),
        "ew1": g["L0_ffn_W1"].transpose(1, 0, 2).reshape(D, E * H),
        "eb1": g["L0_ffn_b1"].reshape(CHUNKS, P).T,
        "ew2": g["L0_ffn_W2"].reshape(CHUNKS, P, D).transpose(1, 0, 2).reshape(P, CHUNKS * D),
        "eb2": eb2.reshape(E * E, E * D),
        "ident": _np.eye(P, dtype=_np.float32),
        "causal": (allowed / _np.maximum(token % T, 1)[None, :]).astype(_np.float32),
        "iota8": _np.tile(_np.arange(E, dtype=_np.float32), (P, 1)),
    }
    arrays = {f"in_{k}": _np.ascontiguousarray(v) for k, v in arrays.items()}
    nc = _bacc.Bacc("TRN2", target_bir_lowering=False, num_devices=1)
    dram = {k[3:]: nc.dram_tensor(k, v.shape, F32, kind="ExternalInput").ap() for k, v in arrays.items()}
    out = nc.dram_tensor("out_0", (TILES, TILE, D), F32, kind="ExternalOutput").ap()
    build(nc, dram, out)
    r = _run(nc, [arrays], core_ids=[0])
    return r.results[0]["out_0"].reshape(B, T, D)
```
